# Optimizing a Trainium2 kernel written in Bass

```python
import numpy as np
import jax
import jax.numpy as jnp

def _softmax(x, axis=-1):
    return jax.nn.softmax(x, axis=axis)

def _gelu(x):
    return jax.nn.gelu(x, approximate=True)

def _silu(x):
    return jax.nn.silu(x)

def _sigmoid(x):
    return jax.nn.sigmoid(x)

def _layernorm(x, axis=-1, eps=1e-05):
    m = jnp.mean(x, axis=axis, keepdims=True)
    v = jnp.var(x, axis=axis, keepdims=True)
    return (x - m) / jnp.sqrt(v + eps)

def _scatter_add(tgt, idx, src, axis=0):
    return tgt.at[idx].add(src)

def _segment_sum(src, seg, n):
    return jax.ops.segment_sum(src, seg, n)
kernel_name = 'mk_vit_tower_d1_tok_img1024_r4_171a2c'

def setup_inputs(seed: int=0):
    np.random.seed(seed)
    _w = jnp.asarray

    def _rec_inputs():
        import jax
        import jax.numpy as jnp
        _rk = jax.random.key(seed)
        x = -4.65018e-05 + 0.999886 * jax.random.normal(jax.random.fold_in(_rk, 1), (64, 3, 112, 112), jnp.float32)
        return x
    x = _rec_inputs()

    def _L0_tok_setup():
        import jax, jax.numpy as jnp
        import numpy as np
        P = 16
        key = jax.random.key(seed)
        k1, k2, k3 = jax.random.split(key, 3)
        B, C, H, W_ = (64, 3, 128, 128)
        D = 256
        x = jax.random.normal(k1, (B, C, H, W_), dtype=jnp.float32)
        W = jax.random.normal(k2, (C * P * P, D), dtype=jnp.float32) * (1.0 / np.sqrt(C * P * P))
        b = jax.random.normal(k3, (D,), dtype=jnp.float32) * 0.01
        return {'x': x, 'W': W, 'b': b}
    _L0_tok_all = _L0_tok_setup()
    _L0_tok_in = {k: v for k, v in _L0_tok_all.items() if k in ('W', 'b')}
    del _L0_tok_all

    def _L0_attn_setup():
        import jax, jax.numpy as jnp
        import numpy as np
        MAX_WAVELENGTH = 10000.0
        NEG_INF = -1000000000.0

        def apply_rope(x):
            S, D = (x.shape[1], x.shape[-1])
            inv_freq = 1.0 / MAX_WAVELENGTH ** (jnp.arange(0, D, 2, dtype=jnp.float32) / D)
            t = jnp.arange(S, dtype=jnp.float32)[:, None] * inv_freq[None, :]
            emb = jnp.concatenate([t, t], axis=-1)
            cos = jnp.cos(emb)[None, :, None, :].astype(x.dtype)
            sin = jnp.sin(emb)[None, :, None, :].astype(x.dtype)
            x1, x2 = jnp.split(x, 2, axis=-1)
            rotated = jnp.concatenate([-x2, x1], axis=-1)
            return x * cos + rotated * sin
        key = jax.random.key(seed)
        k1, k2, k3 = jax.random.split(key, 3)
        B, S, dim = (2, 512, 256)
        x = jax.random.normal(k1, (B, S, dim), dtype=jnp.float32)
        w_qkv = jax.random.normal(k2, (dim, 3 * dim), dtype=jnp.float32) * dim ** (-0.5)
        w_proj = jax.random.normal(k3, (dim, dim), dtype=jnp.float32) * dim ** (-0.5)
        b_proj = jnp.zeros((dim,), dtype=jnp.float32)
        return {'x': x, 'w_qkv': w_qkv, 'w_proj': w_proj, 'b_proj': b_proj}
    _L0_attn_all = _L0_attn_setup()
    _L0_attn_in = {k: v for k, v in _L0_attn_all.items() if k in ('w_qkv', 'w_proj', 'b_proj')}
    del _L0_attn_all

    def _L0_ffn_setup():
        import math
        import jax, jax.numpy as jnp
        import numpy as np
        E = 8
        H = 256
        HP = 128
        SPARSITY = 8
        N_ROTATE = 64
        ROPE_BASE = 10000.0

        def _rope(x, pos):
            half = N_ROTATE // 2
            inv_freq = 1.0 / ROPE_BASE ** (jnp.arange(half, dtype=jnp.float32) * 2.0 / N_ROTATE)
            ang = pos.astype(jnp.float32)[..., None] * inv_freq
            sin, cos = (jnp.sin(ang), jnp.cos(ang))
            x1, x2 = (x[..., :half], x[..., half:])
            return jnp.concatenate([x1 * cos - x2 * sin, x2 * cos + x1 * sin], axis=-1)
        key = jax.random.key(seed)
        k1, k2, k3, k4 = jax.random.split(key, 4)
        B, T = (4, 2048)
        X = jax.random.normal(k1, (B, T, H), dtype=jnp.float32)
        Wr = jax.random.uniform(k2, (E, H), minval=-1 / math.sqrt(H), maxval=1 / math.sqrt(H), dtype=jnp.float32)
        bq = 1 / math.sqrt(3 * HP)
        Wqkv = jax.random.uniform(k3, (E, H, 3 * HP), minval=-bq, maxval=bq, dtype=jnp.float32)
        bo = 1 / math.sqrt(H * E)
        Wo = jax.random.uniform(k4, (E, HP, H), minval=-bo, maxval=bo, dtype=jnp.float32)
        return {'X': X, 'Wr': Wr, 'Wqkv': Wqkv, 'Wo': Wo}
    _L0_ffn_all = _L0_ffn_setup()
    _L0_ffn_in = {k: v for k, v in _L0_ffn_all.items() if k in ('Wr', 'Wqkv', 'Wo')}
    del _L0_ffn_all
    return {'x': x, 'L0_tok_W': _L0_tok_in['W'], 'L0_tok_b': _L0_tok_in['b'], 'L0_attn_w_qkv': _L0_attn_in['w_qkv'], 'L0_attn_w_proj': _L0_attn_in['w_proj'], 'L0_attn_b_proj': _L0_attn_in['b_proj'], 'L0_ffn_Wr': _L0_ffn_in['Wr'], 'L0_ffn_Wqkv': _L0_ffn_in['Wqkv'], 'L0_ffn_Wo': _L0_ffn_in['Wo']}

def reference(x, L0_tok_W, L0_tok_b, L0_attn_w_qkv, L0_attn_w_proj, L0_attn_b_proj, L0_ffn_Wr, L0_ffn_Wqkv, L0_ffn_Wo):
    import jax
    import jax.numpy as jnp

    def _L0_tok_ref(x, W, b):
        import jax, jax.numpy as jnp
        import numpy as np
        P = 16
        B, C, H, W_ = x.shape
        nh, nw = (H // P, W_ // P)
        patches = x.reshape(B, C, nh, P, nw, P)
        patches = patches.transpose(0, 2, 4, 1, 3, 5)
        patches = patches.reshape(B, nh * nw, C * P * P)
        return jnp.einsum('bnk,kd->bnd', patches, W) + b

    def _L0_attn_ref(x, w_qkv, w_proj, b_proj):
        import jax, jax.numpy as jnp
        import numpy as np
        MAX_WAVELENGTH = 10000.0
        NEG_INF = -1000000000.0

        def apply_rope(x):
            S, D = (x.shape[1], x.shape[-1])
            inv_freq = 1.0 / MAX_WAVELENGTH ** (jnp.arange(0, D, 2, dtype=jnp.float32) / D)
            t = jnp.arange(S, dtype=jnp.float32)[:, None] * inv_freq[None, :]
            emb = jnp.concatenate([t, t], axis=-1)
            cos = jnp.cos(emb)[None, :, None, :].astype(x.dtype)
            sin = jnp.sin(emb)[None, :, None, :].astype(x.dtype)
            x1, x2 = jnp.split(x, 2, axis=-1)
            rotated = jnp.concatenate([-x2, x1], axis=-1)
            return x * cos + rotated * sin
        B, S, dim = x.shape
        heads = 16
        head_dim = dim // heads
        scale = head_dim ** (-0.5)
        qkv = x @ w_qkv
        qkv = qkv.reshape(B, S, 3, heads, head_dim)
        Q, K, V = (qkv[:, :, 0], qkv[:, :, 1], qkv[:, :, 2])
        Q = apply_rope(Q)
        K = apply_rope(K)
        attn = jnp.einsum('bqhd,bkhd->bhqk', Q, K) * scale
        causal = jnp.tril(jnp.ones((S, S), dtype=bool))[None, None]
        attn = jnp.where(causal, attn, jnp.asarray(NEG_INF, attn.dtype))
        attn = jax.nn.softmax(attn, axis=-1)
        out = jnp.einsum('bhqk,bkhd->bqhd', attn, V).reshape(B, S, dim)
        return out @ w_proj + b_proj

    def _L0_ffn_ref(X, Wr, Wqkv, Wo):
        import math
        import jax, jax.numpy as jnp
        import numpy as np
        E = 8
        H = 256
        HP = 128
        SPARSITY = 8
        N_ROTATE = 64
        ROPE_BASE = 10000.0

        def _rope(x, pos):
            half = N_ROTATE // 2
            inv_freq = 1.0 / ROPE_BASE ** (jnp.arange(half, dtype=jnp.float32) * 2.0 / N_ROTATE)
            ang = pos.astype(jnp.float32)[..., None] * inv_freq
            sin, cos = (jnp.sin(ang), jnp.cos(ang))
            x1, x2 = (x[..., :half], x[..., half:])
            return jnp.concatenate([x1 * cos - x2 * sin, x2 * cos + x1 * sin], axis=-1)
        B, T, _ = X.shape
        k = min(max(T // SPARSITY, 2), T)
        logits = jax.nn.sigmoid(jnp.einsum('bth,eh->bte', X, Wr))
        topk_vals, topk_I = jax.lax.top_k(logits.transpose(0, 2, 1), k)
        idx_flat = topk_I.reshape(B, E * k)
        Xg = jnp.take_along_axis(X, idx_flat[:, :, None], axis=1).reshape(B, E, k, H)
        QKV = jnp.einsum('beki,eij->bekj', Xg, Wqkv)
        Q, K, V = jnp.split(QKV, 3, axis=-1)
        Q = jnp.concatenate([_rope(Q[..., :N_ROTATE], topk_I), Q[..., N_ROTATE:]], axis=-1)
        K = jnp.concatenate([_rope(K[..., :N_ROTATE], topk_I), K[..., N_ROTATE:]], axis=-1)
        M = topk_I[..., :, None] >= topk_I[..., None, :]
        scores = jnp.einsum('bekd,bemd->bekm', Q, K) / math.sqrt(HP)
        scores = jnp.where(M, scores, -jnp.inf)
        A = jax.nn.softmax(scores, axis=-1)
        AV = jnp.einsum('bekm,bemd->bekd', A, V)
        AV = AV * topk_vals[..., None]
        Xpre = jnp.einsum('bekj,eji->beki', AV, Wo)
        out = jnp.zeros((B, T, H), dtype=X.dtype)
        out = out.at[jnp.arange(B)[:, None], idx_flat].add(Xpre.reshape(B, E * k, H))
        return out
    h = _L0_tok_ref(x, L0_tok_W, L0_tok_b)
    h = h + _L0_attn_ref(_layernorm(h, axis=-1), L0_attn_w_qkv, L0_attn_w_proj, L0_attn_b_proj)
    h = h + _L0_ffn_ref(_layernorm(h, axis=-1), L0_ffn_Wr, L0_ffn_Wqkv, L0_ffn_Wo)
    return h

_drawn_inputs = setup_inputs


def setup_inputs(seed=0):
    import zlib

    import numpy as np

    out = dict(_drawn_inputs(seed))
    spreads = {'L0_attn_b_proj': (0.0, 0.1)}
    factors = {'L0_tok_b': 3.79}
    for name, (base, spread) in spreads.items():
        noise = np.random.default_rng([zlib.crc32(name.encode()), seed]).standard_normal(out[name].shape)
        drawn = base * np.exp(spread * noise) if base else spread * noise
        out[name] = jnp.asarray(drawn.astype(out[name].dtype))
    for name, factor in factors.items():
        out[name] = (out[name] * factor).astype(out[name].dtype)
    return out
```

```python
from contextlib import ExitStack

import concourse.bass as bass
from concourse import mybir

F32 = mybir.dt.float32
ALU = mybir.AluOpType
ACT = mybir.ActivationFunctionType
AX = mybir.AxisListType.X

P = 128
T = 49
TP = 64
IMGS = 2
PAIRS = 32
D = 256
DC = D // P
KC = 768 // P
PATCH_COLS = IMGS * T
HEADS, HD = 16, 16
HC = HEADS // 2
SC = HC * T
EPS = 1e-5
E, HP, SLOTS = 8, 128, 6
ROT = 32
PS = IMGS * SLOTS
NS = PAIRS * PS
GROUP = 8
GS = GROUP * PS
NG = PAIRS // GROUP
QUAD = 4
NQ = PAIRS // QUAD
NEG = -1.0e30

C_ID = 0
C_COS = C_ID + P
C_SIN = C_COS + HD
C_CAUSAL = C_SIN + HD
C_HEAD = C_CAUSAL + T
C_ROT = C_HEAD + HC
C_MASKF = C_ROT + P
C_SLOT = C_MASKF + GS
C_END = C_SLOT + SLOTS


def view(tile, p0, n, off, dims):
    base = tile[p0:p0 + n, bass.ds(off, 1)] if not isinstance(off, int) else tile[p0:p0 + n, off:off + 1]
    return bass.AP(tensor=base.tensor, offset=base.offset, ap=[list(base.ap[0])] + [list(d) for d in dims])


def wait(eng, sem, value):
    if isinstance(value, int) and value <= 0:
        return
    eng.wait_ge(sem, value)


def exists(u, n):
    return not isinstance(u, int) or 0 <= u < n


def run_steps(eng, step, first, loop_from, loop_to, last):
    for t in range(first, loop_from):
        step(t, t % 2)
    with eng.Fori(0, (loop_to - loop_from) // 2) as i:
        for j in range(2):
            step(i * 2 + (loop_from + j), j)
    for t in range(loop_to, last):
        step(t, t % 2)


def build_attention(nc, io, h_all, logits, consts):
    with ExitStack() as ctx:
        def sb(name, cols, rows=P):
            return ctx.enter_context(nc.sbuf_tensor(name, [rows, cols], F32))

        def sem(name):
            return ctx.enter_context(nc.semaphore(name))

        w_tok = sb("w_tok", KC * D)
        w_qkv = sb("w_qkv", DC * 3 * D)
        w_proj = sb("w_proj", DC * D)
        w_router = sb("w_router", DC * E)
        b_tok = sb("b_tok", D)
        b_proj = sb("b_proj", D)
        patches = [sb(f"patches{j}", KC * PATCH_COLS + TP - T) for j in range(2)]
        xn = [sb(f"xn{j}", D) for j in range(2)]
        xn2 = [sb(f"xn2_{j}", D) for j in range(2)]
        xnT = sb("xnT", D)
        xn2T = sb("xn2T", D)
        qk_cos = sb("qk_cos", 2 * D)
        qk_sin = sb("qk_sin", 2 * D)
        qk_rot = sb("qk_rot", 2 * D)
        qkT = sb("qkT", 4 * P)
        k_blocks = sb("k_blocks", DC * IMGS * SC)
        scores = sb("scores", HEADS * T)
        probs = [sb(f"probs{j}", HEADS * TP) for j in range(2)]
        probsT = sb("probsT", 2 * 4 * P)
        v_rows = [sb(f"v_rows{j}", D) for j in range(2)]
        v_blocks = sb("v_blocks", IMGS * HC * 2 * HD)
        attnT = sb("attnT", D)
        row_max = sb("row_max", HEADS)
        row_sum = sb("row_sum", HEADS)
        row_inv = sb("row_inv", HEADS)
        stats = sb("stats", 6)
        stats2 = sb("stats2", 6)
        moments = sb("moments", 2)
        moments2 = sb("moments2", 2)
        var_eps = sb("var_eps", 1)
        var_eps2 = sb("var_eps2", 1)
        rstd = sb("rstd", 1)
        rstd2 = sb("rstd2", 1)
        minus_half = sb("minus_half", 1)
        epsilon = sb("epsilon", 1)
        fence = sb("fence", 2)

        def bank(name):
            return ctx.enter_context(nc.psum_tensor(name, [P, 512], F32))

        p_h = bank("p_h")
        p_xT = bank("p_xT")
        p_qk = bank("p_qk")
        p_v = bank("p_v")
        p_mix = bank("p_mix")
        p_s = ctx.enter_context(nc.psum_tensor("p_s", [P, 1024], F32))
        p_pT = bank("p_pT")

        s_w = sem("s_w")
        s_wqkv = sem("s_wqkv")
        s_zero = sem("s_zero")
        s_pat = [sem(f"s_pat{j}") for j in range(2)]
        s_store = [sem(f"s_store{j}") for j in range(2)]
        pe_h, pe_xT, pe_qk, pe_v, pe_qkT, pe_s, pe_pT, pe_av, pe_proj, pe_x2T, pe_lg = (
            sem(n) for n in ("pe_h", "pe_xT", "pe_qk", "pe_v", "pe_qkT", "pe_s", "pe_pT", "pe_av", "pe_proj",
                             "pe_x2T", "pe_lg"))
        act_xT, act_exp, act_v, act_pT, act_av, act_x2T, act_qkT, act_lg, act_vb = (
            sem(n) for n in ("act_xT", "act_exp", "act_v", "act_pT", "act_av", "act_x2T", "act_qkT", "act_lg",
                             "act_vb"))
        dve_mask, dve_max, dve_shift, dve_rope, dve_xn2, dve_xn, dve_sum, dve_inv = (
            sem(n) for n in ("dve_mask", "dve_max", "dve_shift", "dve_rope", "dve_xn2", "dve_xn", "dve_sum",
                             "dve_inv"))
        dve_res, dve_h2, dve_st2, dve_mom2, dve_h, dve_st, dve_mom = (
            sem(n) for n in ("dve_res", "dve_h2", "dve_st2", "dve_mom2", "dve_h", "dve_st", "dve_mom"))
        pool_rope, pool_kb, pool_norm, pool_eps, pool_rstd, pool_eps2, pool_rstd2 = (
            sem(n) for n in ("pool_rope", "pool_kb", "pool_norm", "pool_eps", "pool_rstd", "pool_eps2",
                             "pool_rstd2"))
        N_ZERO = 7
        LOOP = (-2, 6, 30, PAIRS + 3)
        block = ctx.enter_context(nc.Block())

        @block.sync
        def _(sp):
            def load_patches(u, j):
                wait(sp, pe_h, u - 1)
                sp.dma_start(patches[j][:, 0:KC * PATCH_COLS], io["patchesT"][u]).then_inc(s_pat[j], 16)

            load_patches(0, 0)
            sp.dma_start(w_tok[:].rearrange("p (c n) -> p c n", c=KC),
                         io["L0_tok_W"].rearrange("(c p) n -> p c n", p=P)).then_inc(s_w, 16)
            load_patches(1, 1)
            sp.dma_start(b_tok[:], io["L0_tok_b"].partition_broadcast(P)).then_inc(s_w, 16)
            sp.dma_start(consts[:], io["consts"]).then_inc(s_w, 16)
            sp.dma_start(w_qkv[:].rearrange("p (c n) -> p c n", c=DC),
                         io["L0_attn_w_qkv"].rearrange("(c p) n -> p c n", p=P)).then_inc(s_wqkv, 16)
            sp.dma_start(w_proj[:].rearrange("p (c n) -> p c n", c=DC),
                         io["L0_attn_w_proj"].rearrange("(c p) n -> p c n", p=P)).then_inc(s_wqkv, 16)
            sp.dma_start(b_proj[:], io["L0_attn_b_proj"].partition_broadcast(P)).then_inc(s_wqkv, 16)
            sp.dma_start(w_router[:], io["routerT"]).then_inc(s_wqkv, 16)

            def step(t, j):
                if exists(t - 3, PAIRS):
                    wait(sp, dve_xn2, t - 2)
                    sp.dma_start(io["xn2_dram"][t - 3], xn2[1 - j][:]).then_inc(s_store[1 - j], 16)
                if exists(t + 4, PAIRS):
                    load_patches(t + 4, j)

            run_steps(sp, step, -2, 6, 28, PAIRS + 3)
            for j in range(2):
                sp.wait_ge(s_store[j], 16 * PAIRS // 2)

        @block.tensor
        def _(pe):
            ident = consts[:, C_ID:C_ID + P]
            pe.wait_ge(s_zero, N_ZERO)

            def min_pair(n):
                return min(n, PAIRS) if isinstance(n, int) else n

            def embed(u, j):
                wait(pe, s_pat[j], pair_loads(u, j))
                wait(pe, dve_h, u)
                for c in range(KC):
                    for b in range(IMGS):
                        col = c * PATCH_COLS + b * T
                        last = nc.tensor.matmul(p_h[b * TP:(b + 1) * TP, 0:D], patches[j][:, col:col + TP],
                                                w_tok[:, c * D:(c + 1) * D], start=c == 0, stop=c == KC - 1)
                last.then_inc(pe_h, 1)

            def pair_loads(u, j):
                return (u // 2 + 1) * 16 if isinstance(u, int) else (u - j) * 8 + 16

            def transpose_rows(src, sem_done):
                for c in range(DC):
                    last = nc.tensor.transpose(p_xT[:, c * P:(c + 1) * P], src[:, c * P:(c + 1) * P], ident)
                last.then_inc(sem_done, 1)

            def qkv(u, j):
                wait(pe, dve_xn, u + 1)
                wait(pe, act_lg, u - 3)
                transpose_rows(xn[j], pe_xT)
                wait(pe, act_xT, u + 1)
                wait(pe, dve_res, u - 2)
                for c in range(DC):
                    last = nc.tensor.matmul(p_qk[:], xnT[:, c * P:(c + 1) * P],
                                            w_qkv[:, c * 3 * D:c * 3 * D + 2 * D], start=c == 0, stop=c == DC - 1)
                last.then_inc(pe_qk, 1)
                wait(pe, act_av, u - 2)
                for c in range(DC):
                    last = nc.tensor.matmul(p_v[:, 0:D], xnT[:, c * P:(c + 1) * P],
                                            w_qkv[:, c * 3 * D + 2 * D:(c + 1) * 3 * D],
                                            start=c == 0, stop=c == DC - 1)
                last.then_inc(pe_v, 1)

            def attend(u, j):
                wait(pe, pool_norm, u + 1)
                wait(pe, act_pT, 2 * u)
                wait(pe, act_qkT, min_pair(u + 2))
                for half, dst in enumerate((p_pT, p_mix)):
                    for g in range(4):
                        head = 2 * (4 * half + g)
                        last = nc.tensor.transpose(dst[:, g * P:(g + 1) * P],
                                                   probs[j][:, head * TP:(head + 2) * TP], ident)
                    last.then_inc(pe_pT, 1)
                wait(pe, act_vb, 4 * (u + 1))
                wait(pe, act_v, min_pair(u + 3))
                for half in range(2):
                    wait(pe, act_pT, 2 * u + half + 1)
                    for b in range(IMGS):
                        for g in range(4):
                            col = D + half * P + b * TP
                            vb = (b * HC + 4 * half + g) * 2 * HD
                            last = nc.tensor.matmul(
                                p_v[32 * g:32 * (g + 1), col:col + TP], v_blocks[:, vb:vb + 2 * HD],
                                probsT[:, (4 * half + g) * P + b * TP:(4 * half + g) * P + (b + 1) * TP],
                                start=True, stop=True)
                last.then_inc(pe_av, 1)

            def second_rows(u, j):
                wait(pe, dve_xn2, u + 1)
                wait(pe, act_xT, min_pair(u + 4))
                wait(pe, act_lg, u)
                transpose_rows(xn2[j], pe_x2T)

            def project(u):
                wait(pe, act_av, u + 1)
                wait(pe, dve_rope, min_pair(u + 3) * 2)
                for c in range(DC):
                    last = nc.tensor.matmul(p_qk[:, 0:D], attnT[:, c * P:(c + 1) * P],
                                            w_proj[:, c * D:(c + 1) * D], start=c == 0, stop=c == DC - 1)
                last.then_inc(pe_proj, 1)

            def route(u):
                wait(pe, act_x2T, u + 1)
                for c in range(DC):
                    last = nc.tensor.matmul(p_xT[:, D:D + E], xn2T[:, c * P:(c + 1) * P],
                                            w_router[:, c * E:(c + 1) * E], start=c == 0, stop=c == DC - 1)
                last.then_inc(pe_lg, 1)

            def transpose_qk(u):
                wait(pe, pool_rope, u + 1)
                wait(pe, act_pT, 2 * (u - 1))
                for c in range(4):
                    last = nc.tensor.transpose(p_mix[:, c * P:(c + 1) * P], qk_rot[:, c * P:(c + 1) * P], ident)
                last.then_inc(pe_qkT, 1)

            def score(u):
                wait(pe, act_qkT, u + 1)
                wait(pe, dve_mask, u)
                for c in range(DC):
                    wait(pe, pool_kb, 2 * u + c + 1)
                    for b in range(IMGS):
                        last = nc.tensor.matmul(p_s[b * TP:(b + 1) * TP, c * 512:c * 512 + SC],
                                                qkT[:, c * P + b * TP:c * P + (b + 1) * TP],
                                                k_blocks[:, (c * IMGS + b) * SC:(c * IMGS + b + 1) * SC],
                                                start=True, stop=True)
                    last.then_inc(pe_s, 1)

            def step(t, j):
                if exists(t, PAIRS):
                    if isinstance(t, int) and t == 0:
                        pe.wait_ge(s_wqkv, 16 * 4)
                    qkv(t, j)
                if exists(t - 2, PAIRS):
                    attend(t - 2, j)
                if exists(t - 3, PAIRS):
                    second_rows(t - 3, 1 - j)
                if exists(t - 2, PAIRS):
                    project(t - 2)
                if exists(t - 3, PAIRS):
                    route(t - 3)
                if exists(t, PAIRS):
                    transpose_qk(t)
                if exists(t + 2, PAIRS):
                    embed(t + 2, j)
                if exists(t, PAIRS):
                    score(t)

            pe.wait_ge(s_w, 16 * 3)
            run_steps(pe, step, *LOOP)

        @block.scalar
        def _(act):
            def step(t, j):
                if exists(t, PAIRS):
                    wait(act, pe_xT, t + 1)
                    nc.scalar.copy(xnT[:], p_xT[:, 0:D]).then_inc(act_xT, 1)
                if exists(t - 1, PAIRS):
                    wait(act, dve_shift, t)
                    wait(act, pe_pT, 2 * (t - 2))
                    nc.scalar.activation(view(probs[1 - j], 0, P, 0, [[TP, HEADS], [1, T]]),
                                         view(scores, 0, P, 0, [[T, HEADS], [1, T]]),
                                         ACT.Exp, scale=float(HD) ** -0.5).then_inc(act_exp, 1)
                if exists(t, PAIRS):
                    wait(act, pe_v, t + 1)
                    nc.scalar.copy(v_rows[j][:], p_v[:, 0:D]).then_inc(act_v, 1)
                if exists(t - 2, PAIRS):
                    for half, src in enumerate((p_pT, p_mix)):
                        wait(act, pe_pT, 2 * (t - 2) + half + 1)
                        nc.scalar.copy(probsT[:, half * 512:(half + 1) * 512], src[:]).then_inc(act_pT, 1)
                    wait(act, pe_av, t - 1)
                    nc.scalar.copy(attnT[:], p_v[:, D:2 * D]).then_inc(act_av, 1)
                if exists(t - 3, PAIRS):
                    wait(act, pe_x2T, t - 2)
                    nc.scalar.copy(xn2T[:], p_xT[:, 0:D]).then_inc(act_x2T, 1)
                if exists(t, PAIRS):
                    wait(act, pe_qkT, t + 1)
                    wait(act, pool_kb, 2 * t)
                    nc.scalar.copy(qkT[:], p_mix[:]).then_inc(act_qkT, 1)
                if exists(t - 3, PAIRS):
                    wait(act, pe_lg, t - 2)
                    nc.scalar.copy(logits[:, bass.ds((t - 3) * E, E)], p_xT[:, D:D + E]).then_inc(act_lg, 1)
                if exists(t - 1, PAIRS):
                    wait(act, act_v, t)
                    wait(act, pe_av, t - 1)
                    for half in range(2):
                        for b in range(IMGS):
                            nc.scalar.copy(
                                view(v_blocks, TP * half, TP, b * HC * 2 * HD + half * HD, [[2 * HD, HC], [1, HD]]),
                                view(v_rows[1 - j], TP * b, TP, half * HD, [[2 * HD, HC], [1, HD]]),
                            ).then_inc(act_vb, 1)

            act.wait_ge(s_zero, N_ZERO)
            run_steps(act, step, *LOOP)

        @block.vector
        def _(dve):
            def softmax_shift(u):
                wait(dve, pe_s, 2 * (u + 1))
                wait(dve, act_exp, u)
                nc.vector.tensor_tensor(view(scores, 0, P, 0, [[SC, DC], [T, HC], [1, T]]),
                                        view(p_s, 0, P, 0, [[512, DC], [T, HC], [1, T]]),
                                        view(consts, 0, P, C_CAUSAL, [[0, DC], [0, HC], [1, T]]),
                                        ALU.add).then_inc(dve_mask, 1)
                wait(dve, dve_mask, u + 1)
                nc.vector.tensor_reduce(row_max[:], view(scores, 0, P, 0, [[T, HEADS], [1, T]]), AX,
                                        ALU.max).then_inc(dve_max, 1)
                wait(dve, dve_max, u + 1)
                s3 = view(scores, 0, P, 0, [[T, HEADS], [1, T]])
                nc.vector.tensor_tensor(s3, s3, view(row_max, 0, P, 0, [[1, HEADS], [0, T]]),
                                        ALU.subtract).then_inc(dve_shift, 1)

            def rope(u):
                wait(dve, pe_qk, u + 1)
                wait(dve, pool_rope, u)
                nc.vector.tensor_tensor(view(qk_cos, 0, P, 0, [[HD, 2 * HEADS], [1, HD]]),
                                        view(p_qk, 0, P, 0, [[HD, 2 * HEADS], [1, HD]]),
                                        view(consts, 0, P, C_COS, [[0, 2 * HEADS], [1, HD]]),
                                        ALU.mult).then_inc(dve_rope, 1)
                half = HD // 2
                nc.vector.tensor_tensor(view(qk_sin, 0, P, 0, [[HD, 2 * HEADS], [half, 2], [1, half]]),
                                        view(p_qk, 0, P, half, [[HD, 2 * HEADS], [-half, 2], [1, half]]),
                                        view(consts, 0, P, C_SIN, [[0, 2 * HEADS], [half, 2], [1, half]]),
                                        ALU.mult).then_inc(dve_rope, 1)

            def normalise(u, dst, mom, rs, done):
                nc.vector.tensor_scalar(dst[:], h_all[:, bass.ds(u * D, D)], mom[:, 0:1], rs[:, 0:1],
                                        ALU.subtract, ALU.mult).then_inc(done, 1)

            def step(t, j):
                if exists(t - 1, PAIRS):
                    softmax_shift(t - 1)
                if exists(t, PAIRS):
                    rope(t)
                if exists(t - 3, PAIRS):
                    wait(dve, pool_rstd2, t - 2)
                    wait(dve, pe_x2T, t - 4)
                    wait(dve, s_store[1 - j], stored(t - 5, j))
                    normalise(t - 3, xn2[1 - j], moments2, rstd2, dve_xn2)
                if exists(t + 1, PAIRS):
                    wait(dve, pool_rstd, t + 2)
                    wait(dve, pe_xT, t)
                    normalise(t + 1, xn[1 - j], moments, rstd, dve_xn)
                sums, rest, rows = exists(t - 1, PAIRS), exists(t - 2, PAIRS), exists(t + 2, PAIRS)
                if rest:
                    h_rest = h_all[:, bass.ds((t - 2) * D, D)]
                    wait(dve, pe_proj, t - 1)
                    nc.vector.tensor_tensor(h_rest, p_qk[:, 0:D], h_rest, ALU.add).then_inc(dve_res, 1)
                if sums:
                    wait(dve, act_exp, t)
                    nc.vector.tensor_reduce(row_sum[:], view(probs[1 - j], 0, P, 0, [[TP, HEADS], [1, T]]), AX,
                                            ALU.add).then_inc(dve_sum, 1)
                if rest:
                    wait(dve, dve_res, t - 1)
                    nc.vector.tensor_tensor(h_rest, h_rest, b_proj[:], ALU.add).then_inc(dve_h2, 1)
                if sums:
                    wait(dve, dve_sum, t)
                    wait(dve, pool_norm, t - 1)
                    nc.vector.reciprocal(row_inv[:], row_sum[:]).then_inc(dve_inv, 1)
                if rows:
                    h_rows = h_all[:, bass.ds((t + 2) * D, D)]
                    wait(dve, pe_h, t + 3)
                    nc.vector.tensor_tensor(h_rows, p_h[:, 0:D], b_tok[:], ALU.add).then_inc(dve_h, 1)
                if rest:
                    wait(dve, dve_h2, t - 1)
                if rows:
                    wait(dve, dve_h, t + 3)
                if rest or rows:
                    nc.vector.memset(fence[:, 0:1], 0.0)
                if rest:
                    nc.vector.bn_stats(stats2[:], h_rest).then_inc(dve_st2, 1)
                if rows:
                    nc.vector.bn_stats(stats[:], h_rows).then_inc(dve_st, 1)
                if rest:
                    wait(dve, dve_st2, t - 1)
                    wait(dve, pool_eps2, t - 2)
                if rows:
                    wait(dve, dve_st, t + 3)
                    wait(dve, pool_eps, t + 2)
                if rest or rows:
                    nc.vector.memset(fence[:, 1:2], 0.0)
                if rest:
                    nc.vector.bn_aggr(moments2[:], stats2[:]).then_inc(dve_mom2, 1)
                if rows:
                    nc.vector.bn_aggr(moments[:], stats[:]).then_inc(dve_mom, 1)

            def stored(u, j):
                if isinstance(u, int):
                    return (u // 2 + 1) * 16 if u >= 0 else 0
                return (u - (1 - j)) * 8 + 16

            dve.wait_ge(s_w, 16 * 3)
            dve.wait_ge(s_wqkv, 16 * 4)
            run_steps(dve, step, *LOOP)

        @block.gpsimd
        def _(pool):
            for tile in (v_blocks, probs[0], probs[1]):
                nc.gpsimd.memset(tile[:], 0.0).then_inc(s_zero, 1)
            for tile in patches:
                nc.gpsimd.memset(tile[:, KC * PATCH_COLS:], 0.0).then_inc(s_zero, 1)
            nc.gpsimd.memset(minus_half[:], -0.5).then_inc(s_zero, 1)
            nc.gpsimd.memset(epsilon[:], EPS).then_inc(s_zero, 1)
            pool.wait_ge(s_zero, N_ZERO)
            pool.wait_ge(s_w, 16 * 3)

            def inverse_std(u, mom, ve, rs, s_mom, s_eps, s_rstd, s_used):
                wait(pool, s_mom, u + 1)
                nc.gpsimd.tensor_tensor(ve[:], mom[:, 1:2], epsilon[:], ALU.add).then_inc(s_eps, 1)
                wait(pool, s_eps, u + 1)
                wait(pool, s_used, u)
                nc.gpsimd.tensor_tensor(rs[:], ve[:], minus_half[:], ALU.pow).then_inc(s_rstd, 1)

            def step(t, j):
                if exists(t, PAIRS):
                    wait(pool, dve_rope, 2 * (t + 1))
                    wait(pool, pe_qkT, t)
                    nc.gpsimd.tensor_tensor(qk_rot[:], qk_cos[:], qk_sin[:], ALU.add).then_inc(pool_rope, 1)
                    wait(pool, act_qkT, t + 1)
                    wait(pool, pe_s, 2 * t)
                    for c in range(DC):
                        nc.gpsimd.tensor_tensor(
                            view(k_blocks, 0, P, c * IMGS * SC, [[SC, IMGS], [T, HC], [1, T]]),
                            view(qkT, 0, P, (DC + c) * P, [[TP, IMGS], [0, HC], [1, T]]),
                            view(consts, 0, P, C_HEAD, [[0, IMGS], [1, HC], [0, T]]),
                            ALU.mult).then_inc(pool_kb, 1)
                if exists(t - 1, PAIRS):
                    wait(pool, dve_inv, t)
                    pr = view(probs[1 - j], 0, P, 0, [[TP, HEADS], [1, T]])
                    nc.gpsimd.tensor_tensor(pr, pr, view(row_inv, 0, P, 0, [[1, HEADS], [0, T]]),
                                            ALU.mult).then_inc(pool_norm, 1)
                if exists(t + 2, PAIRS):
                    inverse_std(t + 2, moments, var_eps, rstd, dve_mom, pool_eps, pool_rstd, dve_xn)
                if exists(t - 2, PAIRS):
                    inverse_std(t - 2, moments2, var_eps2, rstd2, dve_mom2, pool_eps2, pool_rstd2, dve_xn2)

            run_steps(pool, step, *LOOP)


def build_routing(nc, logits, consts, gates, chosen, chosen_gate):
    with ExitStack() as ctx:
        def sb(name, cols, rows=P):
            return ctx.enter_context(nc.sbuf_tensor(name, [rows, cols], F32))

        def sem(name):
            return ctx.enter_context(nc.semaphore(name))

        HALVES = 2
        HP_ = PAIRS // HALVES
        SETS = HALVES * IMGS
        gate_rows = sb("gate_rows", SETS * TP)
        code_rows = sb("code_rows", SETS * TP)
        code_cols = sb("code_cols", PAIRS * E)
        top8 = sb("top8", SETS * 8)
        above = sb("above", SETS * T)
        ties = sb("ties", SETS * T)
        tie_rank = sb("tie_rank", SETS * T)
        taken = sb("taken", SETS * T)
        order = sb("order", SETS * T)
        room = sb("room", SETS)
        zeros = sb("zeros", T)
        p_rows = ctx.enter_context(nc.psum_tensor("p_rows", [P, 512], F32))
        p_cols = ctx.enter_context(nc.psum_tensor("p_cols", [P, 512], F32))
        r_exp, r_one, r_gate, r_rowsT, r_rows, r_zero, r_codeT, r_code, r_cols, r_clear, r_chosen, r_sel = (
            sem(n) for n in ("r_exp", "r_one", "r_gate", "r_rowsT", "r_rows", "r_zero", "r_codeT", "r_code",
                             "r_cols", "r_clear", "r_chosen", "r_sel"))
        block = ctx.enter_context(nc.Block())

        @block.scalar
        def _(act):
            nc.scalar.activation(gates[:], logits[:], ACT.Exp, scale=-1.0).then_inc(r_exp, 1)

        @block.tensor
        def _(pe):
            ident = consts[:, C_ID:C_ID + P]
            pe.wait_ge(r_gate, 1)
            for h in range(HALVES):
                last = nc.tensor.transpose(p_rows[:, h * P:(h + 1) * P],
                                           gates[:, h * HP_ * E:(h + 1) * HP_ * E], ident)
            last.then_inc(r_rowsT, 1)
            pe.wait_ge(r_code, SETS)
            for h in range(HALVES):
                last = nc.tensor.transpose(p_cols[:, h * P:(h + 1) * P], code_rows[:, h * P:(h + 1) * P], ident)
            last.then_inc(r_codeT, 1)

        @block.vector
        def _(dve):
            dve.wait_ge(r_exp, 1)
            nc.vector.tensor_scalar(gates[:], gates[:], 1.0, None, ALU.add).then_inc(r_one, 1)
            dve.wait_ge(r_one, 1)
            nc.vector.reciprocal(gates[:], gates[:]).then_inc(r_gate, 1)
            dve.wait_ge(r_rowsT, 1)
            nc.vector.tensor_copy(gate_rows[:], p_rows[:, 0:SETS * TP]).then_inc(r_rows, 1)
            dve.wait_ge(r_rows, 1)
            dve.wait_ge(r_zero, 2)
            done = 0

            def stage(op):
                nonlocal done
                for k in range(SETS):
                    op(k).then_inc(r_sel, 1)
                done += SETS
                dve.wait_ge(r_sel, done)

            def of(tile, k, width=T, pitch=T):
                return tile[:, k * pitch:k * pitch + width]

            stage(lambda k: nc.vector.max(of(top8, k, 8, 8), of(gate_rows, k, T, TP)))
            cut = [top8[:, k * 8 + SLOTS - 1:k * 8 + SLOTS] for k in range(SETS)]
            stage(lambda k: nc.vector.tensor_scalar(of(above, k), of(gate_rows, k, T, TP), cut[k], None, ALU.is_gt))
            stage(lambda k: nc.vector.tensor_scalar(of(ties, k), of(gate_rows, k, T, TP), cut[k], None,
                                                    ALU.is_equal))
            stage(lambda k: nc.vector.tensor_reduce(of(room, k, 1, 1), of(above, k), AX, ALU.add))
            stage(lambda k: nc.vector.tensor_scalar(of(room, k, 1, 1), of(room, k, 1, 1), -1.0, float(SLOTS),
                                                    ALU.mult, ALU.add))
            stage(lambda k: nc.vector.tensor_tensor_scan(of(tie_rank, k), of(ties, k), zeros[:], 0.0,
                                                         ALU.add, ALU.add))
            stage(lambda k: nc.vector.scalar_tensor_tensor(out=of(taken, k), in0=of(tie_rank, k),
                                                           scalar=of(room, k, 1, 1), in1=of(ties, k),
                                                           op0=ALU.is_le, op1=ALU.mult))
            stage(lambda k: nc.vector.tensor_tensor(of(taken, k), of(taken, k), of(above, k), ALU.add))
            stage(lambda k: nc.vector.tensor_tensor_scan(of(order, k), of(taken, k), zeros[:], 0.0,
                                                         ALU.add, ALU.add))
            for k in range(SETS):
                nc.vector.tensor_tensor(of(code_rows, k, T, TP), of(order, k), of(taken, k),
                                        ALU.mult).then_inc(r_code, 1)
            dve.wait_ge(r_codeT, 1)
            nc.vector.tensor_copy(code_cols[:], p_cols[:, 0:PAIRS * E]).then_inc(r_cols, 1)
            dve.wait_ge(r_cols, 1)
            dve.wait_ge(r_clear, 1)
            for b in range(IMGS):
                nc.vector.tensor_tensor(
                    view(chosen, b * TP, TP, b * SLOTS, [[PS, PAIRS * E], [1, SLOTS]]),
                    view(code_cols, b * TP, TP, 0, [[1, PAIRS * E], [0, SLOTS]]),
                    view(consts, b * TP, TP, C_SLOT, [[0, PAIRS * E], [1, SLOTS]]),
                    ALU.is_equal).then_inc(r_chosen, 1)

        @block.gpsimd
        def _(pool):
            nc.gpsimd.memset(code_rows[:], 0.0).then_inc(r_zero, 1)
            nc.gpsimd.memset(zeros[:], 0.0).then_inc(r_zero, 1)
            nc.gpsimd.memset(chosen[:], 0.0).then_inc(r_clear, 1)
            pool.wait_ge(r_chosen, IMGS)
            nc.gpsimd.tensor_tensor(view(chosen_gate, 0, P, 0, [[PS, PAIRS * E], [1, PS]]),
                                    view(chosen, 0, P, 0, [[PS, PAIRS * E], [1, PS]]),
                                    view(gates, 0, P, 0, [[1, PAIRS * E], [0, PS]]), ALU.mult)


def build_gather(nc, io, consts, chosen, slot_rows, slot_angles):
    with ExitStack() as ctx:
        def sem(name):
            return ctx.enter_context(nc.semaphore(name))

        rows = [ctx.enter_context(nc.sbuf_tensor(f"rows{j}", [P, QUAD * D], F32)) for j in range(2)]
        banks = [[ctx.enter_context(nc.psum_tensor(f"p_g{j}{c}", [P, 512], F32)) for c in range(DC + 1)]
                 for j in range(2)]
        g_in = [sem(f"g_in{j}") for j in range(2)]
        g_mm, g_act, g_dve = sem("g_mm"), sem("g_act"), sem("g_dve")
        QC = QUAD * E * PS
        block = ctx.enter_context(nc.Block())

        @block.sync
        def _(sp):
            def load(q, j):
                wait(sp, g_mm, q - 1)
                sp.dma_start(rows[j][:].rearrange("p (q n) -> p q n", q=QUAD),
                             io["xn2_dram"][bass.ds(q * QUAD, QUAD)].rearrange("q p n -> p q n")
                             ).then_inc(g_in[j], 16)

            for j in range(2):
                load(j, j)
            with sp.Fori(0, NQ // 2 - 1) as i:
                for j in range(2):
                    load(i * 2 + (2 + j), j)

        @block.tensor
        def _(pe):
            def gather(i, j):
                q = i * 2 + j
                wait(pe, g_in[j], i * 16 + 16)
                wait(pe, g_act, q - 1)
                wait(pe, g_dve, (q - 1) * 2)
                for k in range(QUAD):
                    for c in range(DC):
                        nc.tensor.matmul(banks[j][c][:, k * E * PS:(k + 1) * E * PS],
                                         rows[j][:, k * D + c * P:k * D + (c + 1) * P],
                                         chosen[:, bass.ds(q * QC + k * E * PS, E * PS)], start=True, stop=True)
                nc.tensor.matmul(banks[j][DC][:, 0:QC], consts[:, C_ROT:C_ROT + P],
                                 chosen[:, bass.ds(q * QC, QC)], start=True, stop=True).then_inc(g_mm, 1)

            for j in range(2):
                gather(0, j)
            with pe.Fori(1, NQ // 2) as i:
                for j in range(2):
                    gather(i, j)

        def spread(copy, dst, base, src, q):
            return copy(view(dst, 0, P, q * (QUAD * PS) + base, [[PS, QUAD], [NS, E], [1, PS]]),
                        view(src, 0, P, 0, [[E * PS, QUAD], [PS, E], [1, PS]]))

        @block.scalar
        def _(act):
            with act.Fori(0, NQ // 2) as i:
                for j in range(2):
                    q = i * 2 + j
                    act.wait_ge(g_mm, q + 1)
                    spread(nc.scalar.copy, slot_rows, 0, banks[j][0], q).then_inc(g_act, 1)

        @block.vector
        def _(dve):
            with dve.Fori(0, NQ // 2) as i:
                for j in range(2):
                    q = i * 2 + j
                    dve.wait_ge(g_mm, q + 1)
                    spread(nc.vector.tensor_copy, slot_rows, E * NS, banks[j][1], q).then_inc(g_dve, 1)
                    spread(nc.vector.tensor_copy, slot_angles, 0, banks[j][2], q).then_inc(g_dve, 1)


def build_experts(nc, io, consts, slot_rows, slot_angles, slot_out):
    with ExitStack() as ctx:
        def sb(name, cols, rows=P):
            return ctx.enter_context(nc.sbuf_tensor(name, [rows, cols], F32))

        def sem(name):
            return ctx.enter_context(nc.semaphore(name))

        x_e = [sb(f"x_e{j}", DC * NS) for j in range(2)]
        w_e = [sb(f"w_e{j}", DC * 3 * HP) for j in range(2)]
        wo_e = [sb(f"wo_e{j}", D) for j in range(4)]
        turned = sb("turned", 2 * NS)
        straight = sb("straight", 2 * NS, 2 * ROT)
        qk = [sb(f"qk{j}", 2 * NS) for j in range(2)]
        v = [sb(f"v{j}", NG * HP, GS) for j in range(4)]
        s_e = sb("s_e", NG * GS, GS)
        a_e = sb("a_e", NG * GS, GS)
        aT = sb("aT", NG * GS, GS)
        avT = sb("avT", NS)
        mx = sb("mx", NG, GS)
        sm = sb("sm", NG, GS)
        inv = sb("inv", NG, GS)
        p_qk = ctx.enter_context(nc.psum_tensor("p_qke", [P, 1024], F32))
        p_v, p_s, p_aT, p_av = (ctx.enter_context(nc.psum_tensor(n, [P, 512], F32))
                                for n in ("p_ve", "p_se", "p_aTe", "p_ave"))
        p_o = ctx.enter_context(nc.psum_tensor("p_oe", [P, 1024], F32))
        e_in = [sem(f"e_in{j}") for j in range(2)]
        e_wo = [sem(f"e_wo{j}") for j in range(2)]
        (m_qk, m_v, m_s, m_aT, m_av, m_o) = (sem(n) for n in ("m_qk", "m_v", "m_s", "m_aT", "m_av", "m_o"))
        (a_rest, a_v, a_exp, a_aT, a_av, a_o) = (sem(n) for n in ("a_rest", "a_v", "a_exp", "a_aT", "a_av", "a_o"))
        (d_turn, d_rope, d_mask, d_max, d_shift, d_sum, d_inv, d_norm, d_o) = (
            sem(n) for n in ("d_turn", "d_rope", "d_mask", "d_max", "d_shift", "d_sum", "d_inv", "d_norm", "d_o"))
        g_s = sem("g_s")
        block = ctx.enter_context(nc.Block())

        def run(eng, step):
            for t in range(E + 2):
                step(t, t % 2)

        @block.sync
        def _(sp):
            for e in range(E):
                j = e % 2
                wait(sp, m_v, e - 1)
                sp.dma_start(x_e[j][:].rearrange("p (c n) -> p c n", c=DC),
                             view(slot_rows, 0, P, e * NS, [[E * NS, DC], [1, NS]])).then_inc(e_in[j], 16)
                sp.dma_start(w_e[j][:].rearrange("p (c n) -> p c n", c=DC),
                             io["L0_ffn_Wqkv"][e].rearrange("(c p) n -> p c n", p=P)).then_inc(e_in[j], 16)
                wait(sp, m_o, e - 3)
                sp.dma_start(wo_e[e % 4][:], io["L0_ffn_Wo"][e]).then_inc(e_wo[j], 16)

        @block.tensor
        def _(pe):
            ident = consts[:, C_ID:C_ID + P]

            def step(t, j):
                if exists(t, E):
                    wait(pe, e_in[j], 32 * (t // 2 + 1))
                    wait(pe, a_rest, t)
                    wait(pe, d_turn, 2 * t)
                    wait(pe, d_rope, 2 * t)
                    for k in range(2):
                        for c in range(DC):
                            last = nc.tensor.matmul(p_qk[:, k * 512:k * 512 + NS],
                                                    w_e[j][:, c * 3 * HP + k * HP:c * 3 * HP + (k + 1) * HP],
                                                    x_e[j][:, c * NS:(c + 1) * NS], start=c == 0, stop=c == DC - 1)
                    last.then_inc(m_qk, 1)
                if exists(t - 1, E):
                    u = t - 1
                    wait(pe, g_s, u + 1)
                    wait(pe, a_rest, u + 1)
                    wait(pe, d_mask, u)
                    for g in range(NG):
                        last = nc.tensor.matmul(p_s[0:GS, g * GS:(g + 1) * GS],
                                                qk[1 - j][:, g * GS:(g + 1) * GS],
                                                qk[1 - j][:, NS + g * GS:NS + (g + 1) * GS], start=True, stop=True)
                    last.then_inc(m_s, 1)
                if exists(t, E):
                    wait(pe, a_v, t)
                    for g in range(NG):
                        for c in range(DC):
                            last = nc.tensor.matmul(p_v[0:GS, g * HP:(g + 1) * HP],
                                                    x_e[j][:, c * NS + g * GS:c * NS + (g + 1) * GS],
                                                    w_e[j][:, c * 3 * HP + 2 * HP:(c + 1) * 3 * HP],
                                                    start=c == 0, stop=c == DC - 1)
                    last.then_inc(m_v, 1)
                if exists(t - 2, E):
                    u = t - 2
                    wait(pe, d_norm, u + 1)
                    wait(pe, a_aT, u)
                    for g in range(NG):
                        last = nc.tensor.transpose(p_aT[0:GS, g * GS:(g + 1) * GS],
                                                   a_e[:, g * GS:(g + 1) * GS], ident[0:GS, 0:GS])
                    last.then_inc(m_aT, 1)
                    wait(pe, a_aT, u + 1)
                    wait(pe, a_av, u)
                    for g in range(NG):
                        last = nc.tensor.matmul(p_av[:, g * GS:(g + 1) * GS], v[u % 4][:, g * HP:(g + 1) * HP],
                                                aT[:, g * GS:(g + 1) * GS], start=True, stop=True)
                    last.then_inc(m_av, 1)
                    wait(pe, a_av, u + 1)
                    wait(pe, e_wo[j], 16 * (u // 2 + 1))
                    wait(pe, a_o, u)
                    wait(pe, d_o, u)
                    for c in range(DC):
                        last = nc.tensor.matmul(p_o[:, c * 512:c * 512 + NS], wo_e[u % 4][:, c * P:(c + 1) * P],
                                                avT[:], start=True, stop=True)
                    last.then_inc(m_o, 1)

            run(pe, step)

        def leave(copy, u, c):
            return copy(view(slot_out, 0, P, (c * E + u) * PS, [[DC * E * PS, PAIRS], [1, PS]]),
                        view(p_o, 0, P, c * 512, [[PS, PAIRS], [1, PS]]))

        @block.scalar
        def _(act):
            def step(t, j):
                if exists(t, E):
                    wait(act, m_qk, t + 1)
                    wait(act, m_s, t - 1)
                    nc.scalar.copy(view(qk[j], 2 * ROT, P - 2 * ROT, 0, [[NS, 2], [1, NS]]),
                                   view(p_qk, 2 * ROT, P - 2 * ROT, 0, [[512, 2], [1, NS]])).then_inc(a_rest, 1)
                if exists(t - 1, E):
                    wait(act, d_shift, t)
                    wait(act, m_aT, t - 1)
                    nc.scalar.activation(a_e[:], s_e[:], ACT.Exp, scale=float(HP) ** -0.5).then_inc(a_exp, 1)
                if exists(t, E):
                    wait(act, m_v, t + 1)
                    nc.scalar.copy(v[t % 4][:], p_v[0:GS, :]).then_inc(a_v, 1)
                if exists(t - 2, E):
                    wait(act, m_aT, t - 1)
                    nc.scalar.copy(aT[:], p_aT[0:GS, 0:NG * GS]).then_inc(a_aT, 1)
                    wait(act, m_av, t - 1)
                    nc.scalar.copy(avT[:], p_av[:, 0:NS]).then_inc(a_av, 1)
                    wait(act, m_o, t - 1)
                    leave(nc.scalar.copy, t - 2, 0).then_inc(a_o, 1)

            run(act, step)

        @block.vector
        def _(dve):
            def step(t, j):
                if exists(t - 1, E):
                    u = t - 1
                    wait(dve, m_s, u + 1)
                    wait(dve, a_exp, u)
                    nc.vector.tensor_tensor(view(s_e, 0, GS, 0, [[GS, NG], [1, GS]]),
                                            view(p_s, 0, GS, 0, [[GS, NG], [1, GS]]),
                                            view(consts, 0, GS, C_MASKF, [[0, NG], [1, GS]]),
                                            ALU.add).then_inc(d_mask, 1)
                    wait(dve, d_mask, u + 1)
                    s3 = view(s_e, 0, GS, 0, [[GS, NG], [1, GS]])
                    nc.vector.tensor_reduce(mx[:], s3, AX, ALU.max).then_inc(d_max, 1)
                    wait(dve, d_max, u + 1)
                    nc.vector.tensor_tensor(s3, s3, view(mx, 0, GS, 0, [[1, NG], [0, GS]]),
                                            ALU.subtract).then_inc(d_shift, 1)
                if exists(t, E):
                    wait(dve, m_qk, t + 1)
                    wait(dve, g_s, t)
                    for lo, hi in ((0, ROT), (ROT, 0)):
                        nc.vector.tensor_tensor(view(turned, lo, ROT, 0, [[NS, 2], [1, NS]]),
                                                view(p_qk, hi, ROT, 0, [[512, 2], [1, NS]]),
                                                view(slot_angles, 2 * ROT + lo, ROT, t * NS, [[0, 2], [1, NS]]),
                                                ALU.mult).then_inc(d_turn, 1)
                    nc.vector.tensor_tensor(view(straight, 0, 2 * ROT, 0, [[NS, 2], [1, NS]]),
                                            view(p_qk, 0, 2 * ROT, 0, [[512, 2], [1, NS]]),
                                            view(slot_angles, 0, 2 * ROT, t * NS, [[0, 2], [1, NS]]),
                                            ALU.mult).then_inc(d_rope, 2)
                if exists(t - 1, E):
                    u = t - 1
                    wait(dve, a_exp, u + 1)
                    a3 = view(a_e, 0, GS, 0, [[GS, NG], [1, GS]])
                    nc.vector.tensor_reduce(sm[:], a3, AX, ALU.add).then_inc(d_sum, 1)
                    wait(dve, d_sum, u + 1)
                    nc.vector.reciprocal(inv[:], sm[:]).then_inc(d_inv, 1)
                    wait(dve, d_inv, u + 1)
                    nc.vector.tensor_tensor(a3, a3, view(inv, 0, GS, 0, [[1, NG], [0, GS]]),
                                            ALU.mult).then_inc(d_norm, 1)
                if exists(t - 2, E):
                    wait(dve, m_o, t - 1)
                    leave(nc.vector.tensor_copy, t - 2, 1).then_inc(d_o, 1)

            run(dve, step)

        @block.gpsimd
        def _(pool):
            for t in range(E):
                wait(pool, d_turn, 2 * (t + 1))
                wait(pool, d_rope, 2 * (t + 1))
                wait(pool, m_s, t - 1)
                nc.gpsimd.tensor_tensor(qk[t % 2][0:2 * ROT, :], straight[:], turned[0:2 * ROT, :],
                                        ALU.add).then_inc(g_s, 1)


def build_scatter(nc, io, consts, h_all, slot_out, chosen_gate):
    with ExitStack() as ctx:
        def sb(name, cols, rows=P):
            return ctx.enter_context(nc.sbuf_tensor(name, [rows, cols], F32))

        def sem(name):
            return ctx.enter_context(nc.semaphore(name))

        ES = E * PS
        outs = [sb(f"outs{j}", QUAD * DC * ES) for j in range(2)]
        gts = [sb(f"gts{j}", QUAD * ES) for j in range(2)]
        back = [sb(f"back{j}", DC * P + P, ES) for j in range(2)]
        final = [sb(f"final{j}", QUAD * D) for j in range(2)]
        p_t = [ctx.enter_context(nc.psum_tensor(f"p_t{j}", [P, 512], F32)) for j in range(2)]
        p_f = [ctx.enter_context(nc.psum_tensor(f"p_f{j}", [P, 512], F32)) for j in range(2)]
        c_in = [sem(f"c_in{j}") for j in range(2)]
        c_out = [sem(f"c_out{j}") for j in range(2)]
        c_T, c_back, c_mm, c_fin = sem("c_T"), sem("c_back"), sem("c_mm"), sem("c_fin")
        block = ctx.enter_context(nc.Block())

        @block.sync
        def _(sp):
            def load(q, j):
                wait(sp, c_T, (q - 1) * QUAD)
                sp.dma_start(outs[j][:], slot_out[:, bass.ds(q * (QUAD * DC * ES), QUAD * DC * ES)]
                             ).then_inc(c_in[j], 16)
                sp.dma_start(gts[j][:], chosen_gate[:, bass.ds(q * (QUAD * ES), QUAD * ES)]).then_inc(c_in[j], 16)

            def store(q, j):
                wait(sp, c_fin, (q + 1) * QUAD)
                for b in range(IMGS):
                    sp.dma_start(io["out"][bass.ds(q * QUAD, QUAD), b].rearrange("q t n -> t q n"),
                                 final[j][b * TP:b * TP + T, :].rearrange("t (q n) -> t q n", q=QUAD)
                                 ).then_inc(c_out[j], 16)

            for j in range(2):
                load(j, j)
            with sp.Fori(0, NQ // 2 - 1) as i:
                for j in range(2):
                    store(i * 2 + j, j)
                    load(i * 2 + (2 + j), j)
            for j in range(2):
                store(NQ - 2 + j, j)
            for j in range(2):
                sp.wait_ge(c_out[j], 16 * IMGS * NQ // 2)

        def quads(eng, body):
            for q in range(2):
                for k in range(QUAD):
                    body(q, q, k, q * QUAD + k)
            with eng.Fori(1, NQ // 2) as i:
                for j in range(2):
                    for k in range(QUAD):
                        q = i * 2 + j
                        body(q, j, k, q * QUAD + k)

        @block.tensor
        def _(pe):
            ident = consts[:, C_ID:C_ID + P]

            def scatter(u, k):
                wait(pe, c_back, u + 1)
                wait(pe, c_fin, u - 1)
                nc.tensor.matmul(p_f[k % 2][:, 0:D], back[k % 2][:, DC * P:], back[k % 2][:, 0:D],
                                 start=True, stop=True).then_inc(c_mm, 1)

            def body(q, j, k, u):
                if k == 0:
                    wait(pe, c_in[j], (q - j) * 16 + 32)
                wait(pe, c_back, u - 1)
                for c in range(DC):
                    nc.tensor.transpose(p_t[k % 2][0:ES, c * P:(c + 1) * P],
                                        outs[j][:, (k * DC + c) * ES:(k * DC + c + 1) * ES], ident)
                nc.tensor.transpose(p_t[k % 2][0:ES, DC * P:DC * P + P], gts[j][:, k * ES:(k + 1) * ES],
                                    ident).then_inc(c_T, 1)
                if not (isinstance(u, int) and u == 0):
                    scatter(u - 1, k - 1)

            quads(pe, body)
            scatter(PAIRS - 1, QUAD - 1)

        @block.scalar
        def _(act):
            def body(q, j, k, u):
                wait(act, c_T, u + 1)
                wait(act, c_mm, u - 1)
                nc.scalar.copy(back[k % 2][:], p_t[k % 2][0:ES, 0:DC * P + P]).then_inc(c_back, 1)

            quads(act, body)

        @block.vector
        def _(dve):
            def body(q, j, k, u):
                wait(dve, c_mm, u + 1)
                if k == 0:
                    wait(dve, c_out[j], (q - j) * 16)
                nc.vector.tensor_tensor(final[j][:, k * D:(k + 1) * D], p_f[k % 2][:, 0:D],
                                        h_all[:, bass.ds(u * D, D)], ALU.add).then_inc(c_fin, 1)

            quads(dve, body)


def build(nc, io):
    with ExitStack() as ctx:
        def sb(name, cols):
            return ctx.enter_context(nc.sbuf_tensor(name, [P, cols], F32))

        consts = sb("consts", C_END)
        h_all = sb("h_all", PAIRS * D)
        logits = sb("logits", PAIRS * E)
        build_attention(nc, io, h_all, logits, consts)
        chosen_gate = sb("chosen_gate", PAIRS * E * PS)
        slot_out = sb("slot_out", PAIRS * DC * E * PS)
        slot_rows = sb("slot_rows", DC * E * NS)
        slot_angles = sb("slot_angles", E * NS)
        with ExitStack() as inner:
            gates = inner.enter_context(nc.sbuf_tensor("gates", [P, PAIRS * E], F32))
            chosen = inner.enter_context(nc.sbuf_tensor("chosen", [P, PAIRS * E * PS], F32))
            build_routing(nc, logits, consts, gates, chosen, chosen_gate)
            build_gather(nc, io, consts, chosen, slot_rows, slot_angles)
        build_experts(nc, io, consts, slot_rows, slot_angles, slot_out)
        build_scatter(nc, io, consts, h_all, slot_out, chosen_gate)


def constants():
    import numpy as np
    c = np.zeros((P, C_END), np.float32)
    row = np.arange(P)
    tok = (row % TP).astype(np.float32)
    c[:, C_ID:C_ID + P] = np.eye(P)
    inv = np.float32(1.0) / np.power(np.float32(10000.0), np.arange(0, HD, 2, dtype=np.float32) / np.float32(HD))
    ang = tok[:, None] * inv.astype(np.float32)[None]
    c[:, C_COS:C_COS + HD] = np.tile(np.cos(ang), 2)
    c[:, C_SIN:C_SIN + HD] = np.concatenate([-np.sin(ang), np.sin(ang)], 1)
    c[:, C_CAUSAL:C_CAUSAL + T] = np.where(np.arange(T)[None] <= (row % TP)[:, None], 0.0, NEG)
    c[:, C_HEAD:C_HEAD + HC] = (row // HD)[:, None] == np.arange(HC)[None]
    inv = np.float32(1.0) / np.power(np.float32(10000.0),
                                     np.arange(ROT, dtype=np.float32) * np.float32(2.0) / np.float32(2 * ROT))
    ang = tok[:, None] * inv.astype(np.float32)[None]
    c[:, C_ROT:C_ROT + P] = np.concatenate([np.cos(ang), np.cos(ang), -np.sin(ang), np.sin(ang)], 1)
    q, k = np.arange(P)[:, None], np.arange(GS)[None]
    c[:, C_MASKF:C_MASKF + GS] = np.where((q // SLOTS == k // SLOTS) & (k <= q), 0.0, NEG)
    c[:, C_SLOT:C_SLOT + SLOTS] = np.arange(1, SLOTS + 1)
    return c


def kernel(x, L0_tok_W, L0_tok_b, L0_attn_w_qkv, L0_attn_w_proj, L0_attn_b_proj, L0_ffn_Wr, L0_ffn_Wqkv, L0_ffn_Wo):
    import numpy as np
    import concourse.bacc as bacc
    from concourse.bass_utils import run_bass_kernel_spmd

    nc = bacc.Bacc("TRN2", target_bir_lowering=False, num_devices=1)
    xs = np.asarray(x).reshape(PAIRS, IMGS, 3, 7, 16, 7, 16).transpose(0, 2, 4, 6, 1, 3, 5)
    xs = xs.reshape(PAIRS, KC, P, PATCH_COLS).transpose(0, 2, 1, 3).reshape(PAIRS, P, KC * PATCH_COLS)
    router = np.asarray(L0_ffn_Wr).T.reshape(DC, P, E).transpose(1, 0, 2).reshape(P, DC * E)
    arrays = {"patchesT": xs, "routerT": router, "consts": constants(), "L0_tok_W": L0_tok_W, "L0_tok_b": L0_tok_b,
              "L0_attn_w_qkv": L0_attn_w_qkv, "L0_attn_w_proj": L0_attn_w_proj, "L0_attn_b_proj": L0_attn_b_proj,
              "L0_ffn_Wqkv": L0_ffn_Wqkv, "L0_ffn_Wo": L0_ffn_Wo}
    arrays = {n: np.ascontiguousarray(a) for n, a in arrays.items()}
    io = {n: nc.dram_tensor("in_" + n, a.shape, mybir.dt.from_np(a.dtype), kind="ExternalInput").ap()
          for n, a in arrays.items()}
    io["xn2_dram"] = nc.dram_tensor("xn2_dram", (PAIRS, P, D), F32, kind="Internal").ap()
    out = nc.dram_tensor("out_rows", (PAIRS, IMGS, T, D), F32, kind="ExternalOutput").ap()
    io["out"] = out
    build(nc, io)
    r = run_bass_kernel_spmd(nc, [{"in_" + n: a for n, a in arrays.items()}], core_ids=[0])
    return r.results[0]["out_rows"].reshape(PAIRS * IMGS, T, D)
```

```python
from contextlib import ExitStack

import concourse.bass as bass
from concourse import mybir

F32 = mybir.dt.float32
F32R = mybir.dt.float32r
ALU = mybir.AluOpType
ACT = mybir.ActivationFunctionType
AX = mybir.AxisListType.X

P = 128
T = 49
TP = 64
IMGS = 2
PAIRS = 32
D = 256
DC = D // P
KC = 768 // P
PATCH_COLS = IMGS * T
HEADS, HD = 16, 16
HC = HEADS // 2
SC = HC * T
EPS = 1e-5
E, HP, SLOTS = 8, 128, 6
ROT = 32
PS = IMGS * SLOTS
NS = PAIRS * PS
GROUP = 8
GS = GROUP * PS
NG = PAIRS // GROUP
QUAD = 4
NQ = PAIRS // QUAD
NEG = -1.0e30

C_ID = 0
C_COS = C_ID + P
C_SIN = C_COS + HD
C_CAUSAL = C_SIN + HD
C_HEAD = C_CAUSAL + T
C_ROT = C_HEAD + HC
C_MASKF = C_ROT + P
C_SLOT = C_MASKF + GS
C_END = C_SLOT + SLOTS


def view(tile, p0, n, off, dims, dtype=None):
    base = tile[p0:p0 + n, bass.ds(off, 1)] if not isinstance(off, int) else tile[p0:p0 + n, off:off + 1]
    if dtype is not None:
        base = base.bitcast(dtype)
    return bass.AP(tensor=base.tensor, offset=base.offset, ap=[list(base.ap[0])] + [list(d) for d in dims])


def wait(eng, sem, value):
    if isinstance(value, int) and value <= 0:
        return
    eng.wait_ge(sem, value)


def pair_loads(u, j):
    return (u // 2 + 1) * 16 if isinstance(u, int) else (u - j) * 8 + 16


def three_passes(w, x):
    return ((w[0], x[0]), (w[1], x[0]), (w[0], x[1]))


def exists(u, n):
    return not isinstance(u, int) or 0 <= u < n


def run_steps(eng, step, first, loop_from, loop_to, last):
    for t in range(first, loop_from):
        step(t, t % 2)
    with eng.Fori(0, (loop_to - loop_from) // 2) as i:
        for j in range(2):
            step(i * 2 + (loop_from + j), j)
    for t in range(loop_to, last):
        step(t, t % 2)


def build_attention(nc, io, h_all, logits, consts):
    with ExitStack() as ctx:
        def sb(name, cols, dtype=F32):
            return ctx.enter_context(nc.sbuf_tensor(name, [P, cols], dtype))

        def parts(name, cols):
            return sb(name + "_hi", cols, F32R), sb(name + "_lo", cols, F32R)

        def sem(name):
            return ctx.enter_context(nc.semaphore(name))

        w_tok = sb("w_tok", KC * D)
        w_tok_parts = parts("w_tok", KC * D)
        w_qkv_parts = parts("w_qkv", DC * 3 * D)
        patch_parts = [parts(f"patch{j}", KC * P) for j in range(2)]
        xnT_parts = parts("xnT", D)
        w_qkv = sb("w_qkv", DC * 3 * D)
        w_proj = sb("w_proj", DC * D)
        w_router = sb("w_router", DC * E)
        b_tok = sb("b_tok", D)
        b_proj = sb("b_proj", D)
        patches = [sb(f"patches{j}", KC * PATCH_COLS) for j in range(2)]
        xn = [sb(f"xn{j}", D) for j in range(2)]
        xn2 = [sb(f"xn2_{j}", D) for j in range(2)]
        xn2T = sb("xn2T", D)
        qk_cos = sb("qk_cos", 2 * D)
        qk_sin = sb("qk_sin", 2 * D)
        qk_rot = sb("qk_rot", 2 * D)
        qkT = sb("qkT", 4 * P)
        k_blocks = sb("k_blocks", DC * IMGS * SC)
        scores = sb("scores", HEADS * T)
        probs = [sb(f"probs{j}", HEADS * TP) for j in range(2)]
        probsT = sb("probsT", 2 * 4 * P)
        v_rows = [sb(f"v_rows{j}", D) for j in range(2)]
        v_blocks = sb("v_blocks", IMGS * HC * 2 * HD)
        attnT = sb("attnT", D)
        row_max = sb("row_max", HEADS)
        row_sum = sb("row_sum", HEADS)
        row_inv = sb("row_inv", HEADS)
        stats = sb("stats", 6)
        stats2 = sb("stats2", 6)
        moments = sb("moments", 2)
        moments2 = sb("moments2", 2)
        var_eps = sb("var_eps", 1)
        var_eps2 = sb("var_eps2", 1)
        rstd = sb("rstd", 1)
        rstd2 = sb("rstd2", 1)
        minus_half = sb("minus_half", 1)
        fences = sb("fences", 4)

        def bank(name):
            return ctx.enter_context(nc.psum_tensor(name, [P, 512], F32))

        p_h = bank("p_h")
        p_xT = bank("p_xT")
        p_qk = bank("p_qk")
        p_v = bank("p_v")
        p_mix = bank("p_mix")
        p_s = ctx.enter_context(nc.psum_tensor("p_s", [P, 1024], F32))
        p_pT = bank("p_pT")

        s_wtok, s_w, s_wq, s_wqkv = (sem(n) for n in ("s_wtok", "s_w", "s_wq", "s_wqkv"))
        s_zero = sem("s_zero")
        s_pat = [sem(f"s_pat{j}") for j in range(2)]
        s_store = [sem(f"s_store{j}") for j in range(2)]
        pe_h, pe_xT, pe_qk, pe_v, pe_qkT, pe_s, pe_pT, pe_av, pe_proj, pe_x2T, pe_lg = (
            sem(n) for n in ("pe_h", "pe_xT", "pe_qk", "pe_v", "pe_qkT", "pe_s", "pe_pT", "pe_av", "pe_proj",
                             "pe_x2T", "pe_lg"))
        act_whi, act_phi, dve_wlo, dve_xlo, pool_plo, pool_bias = (
            sem(n) for n in ("act_whi", "act_phi", "dve_wlo", "dve_xlo", "pool_plo", "pool_bias"))
        act_xT, act_exp, act_v, act_pT, act_av, act_x2T, act_qkT, act_lg, act_vb = (
            sem(n) for n in ("act_xT", "act_exp", "act_v", "act_pT", "act_av", "act_x2T", "act_qkT", "act_lg",
                             "act_vb"))
        dve_mask, dve_max, dve_shift, dve_rope, dve_rot, dve_xn2, dve_xn, dve_sum, dve_inv = (
            sem(n) for n in ("dve_mask", "dve_max", "dve_shift", "dve_rope", "dve_rot", "dve_xn2", "dve_xn", "dve_sum",
                             "dve_inv"))
        dve_res, dve_st2, dve_mom2, dve_h, dve_st, dve_mom = (
            sem(n) for n in ("dve_res", "dve_st2", "dve_mom2", "dve_h", "dve_st", "dve_mom"))
        pool_kb, pool_norm, pool_rstd, pool_rstd2, dve_eps, dve_eps2 = (
            sem(n) for n in ("pool_kb", "pool_norm", "pool_rstd", "pool_rstd2", "dve_eps", "dve_eps2"))
        N_ZERO = 8
        LOOP = (-2, 6, 30, PAIRS + 3)
        block = ctx.enter_context(nc.Block())

        @block.sync
        def _(sp):
            def load_patches(u, j):
                wait(sp, pool_plo, u - 1)
                sp.dma_start(patches[j][:], io["patchesT"][u]).then_inc(s_pat[j], 16)

            load_patches(0, 0)
            sp.dma_start(w_tok[:].rearrange("p (c n) -> p c n", c=KC),
                         io["L0_tok_W"].rearrange("(c p) n -> p c n", p=P)).then_inc(s_wtok, 16)
            load_patches(1, 1)
            sp.dma_start(b_tok[:], io["L0_tok_b"].partition_broadcast(P)).then_inc(s_w, 16)
            sp.dma_start(consts[:], io["consts"]).then_inc(s_w, 16)
            sp.dma_start(w_qkv[:].rearrange("p (c n) -> p c n", c=DC),
                         io["L0_attn_w_qkv"].rearrange("(c p) n -> p c n", p=P)).then_inc(s_wq, 16)
            sp.dma_start(w_proj[:].rearrange("p (c n) -> p c n", c=DC),
                         io["L0_attn_w_proj"].rearrange("(c p) n -> p c n", p=P)).then_inc(s_wqkv, 16)
            sp.dma_start(b_proj[:], io["L0_attn_b_proj"].partition_broadcast(P)).then_inc(s_wqkv, 16)
            sp.dma_start(w_router[:], io["routerT"]).then_inc(s_wqkv, 16)

            def step(t, j):
                if exists(t - 3, PAIRS):
                    wait(sp, dve_xn2, t - 2)
                    sp.dma_start(io["xn2_dram"][t - 3], xn2[1 - j][:]).then_inc(s_store[1 - j], 16)
                if exists(t + 4, PAIRS):
                    load_patches(t + 4, j)

            run_steps(sp, step, -2, 6, 28, PAIRS + 3)
            for j in range(2):
                sp.wait_ge(s_store[j], 16 * PAIRS // 2)

        @block.tensor
        def _(pe):
            ident = consts[:, C_ID:C_ID + P]
            pe.wait_ge(s_zero, N_ZERO)

            def min_pair(n):
                return min(n, PAIRS) if isinstance(n, int) else n

            def embed(u, j):
                wait(pe, act_phi, u + 1)
                wait(pe, pool_plo, u + 1)
                wait(pe, dve_h, u)
                wait(pe, dve_res, u - 4)
                for n, (w, x) in enumerate(three_passes(w_tok_parts, patch_parts[j])):
                    for c in range(KC):
                        last = nc.tensor.matmul(p_h[:, 0:D], x[:, c * P:(c + 1) * P], w[:, c * D:(c + 1) * D],
                                                start=n == 0 and c == 0, stop=n == 2 and c == KC - 1)
                last.then_inc(pe_h, 1)

            def transpose_rows(src, sem_done):
                for c in range(DC):
                    last = nc.tensor.transpose(p_xT[:, c * P:(c + 1) * P], src[:, c * P:(c + 1) * P], ident)
                last.then_inc(sem_done, 1)

            def first_rows(u, j):
                wait(pe, dve_xn, u + 1)
                wait(pe, act_x2T, u - 3)
                transpose_rows(xn[j], pe_xT)

            def qkv(u):
                wait(pe, act_xT, u + 1)
                wait(pe, dve_rope, 2 * u)
                for n, (w, x) in enumerate(three_passes(w_qkv_parts, xnT_parts)):
                    if n == 2:
                        wait(pe, dve_xlo, u + 1)
                    for c in range(DC):
                        last = nc.tensor.matmul(p_qk[:], x[:, c * P:(c + 1) * P],
                                                w[:, c * 3 * D:c * 3 * D + 2 * D],
                                                start=n == 0 and c == 0, stop=n == 2 and c == DC - 1)
                last.then_inc(pe_qk, 1)
                wait(pe, act_av, u - 2)
                for n, (w, x) in enumerate(three_passes(w_qkv_parts, xnT_parts)):
                    for c in range(DC):
                        last = nc.tensor.matmul(p_v[:, 0:D], x[:, c * P:(c + 1) * P],
                                                w[:, c * 3 * D + 2 * D:(c + 1) * 3 * D],
                                                start=n == 0 and c == 0, stop=n == 2 and c == DC - 1)
                last.then_inc(pe_v, 1)

            def transpose_probs(u, j):
                wait(pe, act_pT, 2 * u)
                wait(pe, act_qkT, min_pair(u + 2))
                for half, dst in enumerate((p_pT, p_mix)):
                    wait(pe, pool_norm, 2 * u + half + 1)
                    for g in range(4):
                        head = 2 * (4 * half + g)
                        last = nc.tensor.transpose(dst[:, g * P:(g + 1) * P],
                                                   probs[j][:, head * TP:(head + 2) * TP], ident)
                    last.then_inc(pe_pT, 1)

            def attend(u):
                wait(pe, act_vb, 4 * (u + 1))
                wait(pe, act_v, min_pair(u + 3))
                for half in range(2):
                    wait(pe, act_pT, 2 * u + half + 1)
                    for b in range(IMGS):
                        for g in range(4):
                            col = D + half * P + b * TP
                            vb = (b * HC + 4 * half + g) * 2 * HD
                            last = nc.tensor.matmul(
                                p_v[32 * g:32 * (g + 1), col:col + TP], v_blocks[:, vb:vb + 2 * HD],
                                probsT[:, (4 * half + g) * P + b * TP:(4 * half + g) * P + (b + 1) * TP],
                                start=True, stop=True)
                last.then_inc(pe_av, 1)

            def second_rows(u, j):
                wait(pe, dve_xn2, u + 1)
                wait(pe, dve_xlo, min_pair(u + 4))
                transpose_rows(xn2[j], pe_x2T)

            def project(u):
                wait(pe, act_av, u + 1)
                wait(pe, dve_h, min_pair(u + 5))
                for c in range(DC):
                    last = nc.tensor.matmul(p_h[:, D:2 * D], attnT[:, c * P:(c + 1) * P],
                                            w_proj[:, c * D:(c + 1) * D], start=c == 0, stop=c == DC - 1)
                last.then_inc(pe_proj, 1)

            def route(u):
                wait(pe, act_x2T, u + 1)
                wait(pe, act_lg, u)
                wait(pe, dve_mask, 2 * min_pair(u + 3) - 1)
                for c in range(DC):
                    last = nc.tensor.matmul(p_s[:, SC:SC + E], xn2T[:, c * P:(c + 1) * P],
                                            w_router[:, c * E:(c + 1) * E], start=c == 0, stop=c == DC - 1)
                last.then_inc(pe_lg, 1)

            def transpose_qk(u):
                wait(pe, dve_rot, u + 1)
                wait(pe, act_pT, 2 * (u - 1))
                for c in range(4):
                    last = nc.tensor.transpose(p_mix[:, c * P:(c + 1) * P], qk_rot[:, c * P:(c + 1) * P], ident)
                last.then_inc(pe_qkT, 1)

            def score(u):
                wait(pe, act_qkT, u + 1)
                wait(pe, act_lg, u - 2)
                for c in range(DC):
                    wait(pe, dve_mask, 2 * u - 1 + c)
                    wait(pe, pool_kb, 2 * u + c + 1)
                    for b in range(IMGS):
                        last = nc.tensor.matmul(p_s[b * TP:(b + 1) * TP, c * 512:c * 512 + SC],
                                                qkT[:, c * P + b * TP:c * P + (b + 1) * TP],
                                                k_blocks[:, (c * IMGS + b) * SC:(c * IMGS + b + 1) * SC],
                                                start=True, stop=True)
                    last.then_inc(pe_s, 1)

            def step(t, j):
                if exists(t, PAIRS):
                    first_rows(t, j)
                if exists(t - 3, PAIRS):
                    project(t - 3)
                if exists(t, PAIRS):
                    if isinstance(t, int) and t == 0:
                        pe.wait_ge(act_whi, 2)
                        pe.wait_ge(dve_wlo, 2)
                        pe.wait_ge(s_wqkv, 16 * 3)
                    qkv(t)
                if exists(t - 2, PAIRS):
                    transpose_probs(t - 2, j)
                if exists(t - 1, PAIRS):
                    score(t - 1)
                if exists(t - 2, PAIRS):
                    attend(t - 2)
                if exists(t, PAIRS):
                    transpose_qk(t)
                if exists(t - 3, PAIRS):
                    second_rows(t - 3, 1 - j)
                if exists(t + 2, PAIRS):
                    embed(t + 2, j)
                if exists(t - 3, PAIRS):
                    route(t - 3)

            pe.wait_ge(s_w, 16 * 2)
            pe.wait_ge(act_whi, 1)
            pe.wait_ge(dve_wlo, 1)
            run_steps(pe, step, *LOOP)

        @block.scalar
        def _(act):
            def patches_high(u, j):
                wait(act, s_pat[j], pair_loads(u, j))
                wait(act, pe_h, u - 1)
                nc.scalar.copy(view(patch_parts[j][0], 0, P, 0, [[P, KC], [TP, IMGS], [1, T]]),
                               view(patches[j], 0, P, 0, [[PATCH_COLS, KC], [T, IMGS], [1, T]])
                               ).then_inc(act_phi, 1)

            def step(t, j):
                if exists(t, PAIRS):
                    wait(act, pe_xT, t + 1)
                    wait(act, pe_v, t)
                    wait(act, dve_xlo, t)
                    nc.scalar.copy(xnT_parts[0][:], p_xT[:, 0:D]).then_inc(act_xT, 1)
                if exists(t + 3, PAIRS) and not (isinstance(t, int) and t < -1):
                    patches_high(t + 3, 1 - j)
                if exists(t, PAIRS):
                    wait(act, pe_v, t + 1)
                    nc.scalar.copy(v_rows[j][:], p_v[:, 0:D]).then_inc(act_v, 1)
                if exists(t - 2, PAIRS):
                    for half, src in enumerate((p_pT, p_mix)):
                        wait(act, pe_pT, 2 * (t - 2) + half + 1)
                        nc.scalar.copy(probsT[:, half * 512:(half + 1) * 512], src[:]).then_inc(act_pT, 1)
                    wait(act, pe_av, t - 1)
                    nc.scalar.copy(attnT[:], p_v[:, D:2 * D]).then_inc(act_av, 1)
                if exists(t, PAIRS):
                    wait(act, pe_qkT, t + 1)
                    wait(act, pool_kb, 2 * t)
                    nc.scalar.copy(qkT[:], p_mix[:]).then_inc(act_qkT, 1)
                if exists(t - 3, PAIRS):
                    wait(act, pe_x2T, t - 2)
                    nc.scalar.copy(xn2T[:], p_xT[:, 0:D]).then_inc(act_x2T, 1)
                if exists(t - 1, PAIRS):
                    wait(act, act_v, t)
                    wait(act, pe_av, t - 1)
                    for half in range(2):
                        for b in range(IMGS):
                            nc.scalar.copy(
                                view(v_blocks, TP * half, TP, b * HC * 2 * HD + half * HD, [[2 * HD, HC], [1, HD]]),
                                view(v_rows[1 - j], TP * b, TP, half * HD, [[2 * HD, HC], [1, HD]]),
                            ).then_inc(act_vb, 1)
                    for c in range(DC):
                        wait(act, dve_shift, 2 * (t - 1) + c + 1)
                        wait(act, pe_pT, 2 * (t - 3) + c + 1)
                        nc.scalar.activation(view(probs[1 - j], 0, P, c * HC * TP, [[TP, HC], [1, T]]),
                                             view(scores, 0, P, c * SC, [[T, HC], [1, T]]),
                                             ACT.Exp, scale=float(HD) ** -0.5).then_inc(act_exp, 1)
                if exists(t - 3, PAIRS):
                    wait(act, pe_lg, t - 2)
                    nc.scalar.copy(logits[:, bass.ds((t - 3) * E, E)], p_s[:, SC:SC + E]).then_inc(act_lg, 1)

            act.wait_ge(s_zero, N_ZERO)
            patches_high(0, 0)
            act.wait_ge(s_wtok, 16)
            nc.scalar.copy(w_tok_parts[0][:], w_tok[:]).then_inc(act_whi, 1)
            patches_high(1, 1)
            act.wait_ge(s_wq, 16)
            nc.scalar.copy(w_qkv_parts[0][:], w_qkv[:]).then_inc(act_whi, 1)
            run_steps(act, step, -2, 6, 28, PAIRS + 3)

        @block.vector
        def _(dve):
            def softmax_shift(u):
                for c in range(DC):
                    wait(dve, pe_s, 2 * u + c + 1)
                    wait(dve, act_exp, 2 * u - 1 + c)
                    nc.vector.tensor_tensor(view(scores, 0, P, c * SC, [[T, HC], [1, T]]),
                                            view(p_s, 0, P, c * 512, [[T, HC], [1, T]]),
                                            view(consts, 0, P, C_CAUSAL, [[0, HC], [1, T]]),
                                            ALU.add).then_inc(dve_mask, 1)
                wait(dve, dve_mask, 2 * (u + 1))
                nc.vector.tensor_reduce(row_max[:], view(scores, 0, P, 0, [[T, HEADS], [1, T]]), AX,
                                        ALU.max).then_inc(dve_max, 1)
                wait(dve, dve_max, u + 1)
                for c in range(DC):
                    s3 = view(scores, 0, P, c * SC, [[T, HC], [1, T]])
                    nc.vector.tensor_tensor(s3, s3, view(row_max, 0, P, c * HC, [[1, HC], [0, T]]),
                                            ALU.subtract).then_inc(dve_shift, 1)

            def rope_cos(u):
                wait(dve, pe_qk, u + 1)
                nc.vector.tensor_tensor(view(qk_cos, 0, P, 0, [[HD, 2 * HEADS], [1, HD]]),
                                        view(p_qk, 0, P, 0, [[HD, 2 * HEADS], [1, HD]]),
                                        view(consts, 0, P, C_COS, [[0, 2 * HEADS], [1, HD]]),
                                        ALU.mult).then_inc(dve_rope, 1)

            def rope_sin(u):
                half = HD // 2
                nc.vector.tensor_tensor(view(qk_sin, 0, P, 0, [[HD, 2 * HEADS], [half, 2], [1, half]]),
                                        view(p_qk, 0, P, half, [[HD, 2 * HEADS], [-half, 2], [1, half]]),
                                        view(consts, 0, P, C_SIN, [[0, 2 * HEADS], [half, 2], [1, half]]),
                                        ALU.mult).then_inc(dve_rope, 1)

            def add_eps(u, mom, ve, s_mom, s_eps, s_used):
                wait(dve, s_mom, u + 1)
                wait(dve, s_used, u)
                nc.vector.tensor_scalar(ve[:], mom[:, 1:2], EPS, None, ALU.add).then_inc(s_eps, 1)

            def rope_add(u):
                wait(dve, dve_rope, 2 * (u + 1))
                wait(dve, pe_qkT, u)
                nc.vector.tensor_tensor(qk_rot[:], qk_cos[:], qk_sin[:], ALU.add).then_inc(dve_rot, 1)

            def fence(col):
                nc.vector.memset(fences[:, col:col + 1], 0.0)

            def normalise(u, dst, mom, rs, done):
                nc.vector.tensor_scalar(dst[:], h_all[:, bass.ds(u * D, D)], mom[:, 0:1], rs[:, 0:1],
                                        ALU.subtract, ALU.mult).then_inc(done, 1)

            def step(t, j):
                if exists(t - 3, PAIRS):
                    h_rest = h_all[:, bass.ds((t - 3) * D, D)]
                    wait(dve, pe_proj, t - 2)
                    wait(dve, pool_bias, t - 2)
                    nc.vector.tensor_tensor(h_rest, p_h[:, D:2 * D], h_rest, ALU.add).then_inc(dve_res, 1)
                    wait(dve, dve_res, t - 2)
                    fence(0)
                    nc.vector.bn_stats(stats2[:], h_rest).then_inc(dve_st2, 1)
                if exists(t, PAIRS):
                    rope_cos(t)
                if exists(t - 3, PAIRS):
                    wait(dve, dve_st2, t - 2)
                    fence(1)
                    nc.vector.bn_aggr(moments2[:], stats2[:]).then_inc(dve_mom2, 1)
                if exists(t, PAIRS):
                    rope_sin(t)
                if exists(t - 3, PAIRS):
                    add_eps(t - 3, moments2, var_eps2, dve_mom2, dve_eps2, pool_rstd2)
                if exists(t, PAIRS):
                    rope_add(t)
                if exists(t - 3, PAIRS):
                    wait(dve, pool_rstd2, t - 2)
                    wait(dve, pe_x2T, t - 4)
                    wait(dve, s_store[1 - j], stored(t - 5, j))
                    normalise(t - 3, xn2[1 - j], moments2, rstd2, dve_xn2)
                if exists(t - 1, PAIRS):
                    softmax_shift(t - 1)
                if exists(t + 1, PAIRS):
                    wait(dve, pool_rstd, t + 2)
                    wait(dve, pe_xT, t)
                    normalise(t + 1, xn[1 - j], moments, rstd, dve_xn)
                if exists(t + 2, PAIRS):
                    h_rows = h_all[:, bass.ds((t + 2) * D, D)]
                    wait(dve, pe_h, t + 3)
                    nc.vector.tensor_tensor(h_rows, p_h[:, 0:D], b_tok[:], ALU.add).then_inc(dve_h, 1)
                if exists(t - 1, PAIRS):
                    for c in range(DC):
                        wait(dve, act_exp, 2 * (t - 1) + c + 1)
                        nc.vector.tensor_reduce(row_sum[:, c * HC:(c + 1) * HC],
                                                view(probs[1 - j], 0, P, c * HC * TP, [[TP, HC], [1, T]]), AX,
                                                ALU.add).then_inc(dve_sum, 1)
                if exists(t - 1, PAIRS):
                    wait(dve, dve_sum, 2 * t)
                    wait(dve, pool_norm, 2 * (t - 1))
                    nc.vector.reciprocal(row_inv[:], row_sum[:]).then_inc(dve_inv, 1)
                if exists(t + 1, PAIRS):
                    wait(dve, act_xT, t + 2)
                    wait(dve, pe_v, t + 1)
                    nc.vector.tensor_tensor(xnT_parts[1][:], p_xT[:, 0:D], xnT_parts[0][:].bitcast(F32),
                                            ALU.subtract).then_inc(dve_xlo, 1)
                if exists(t + 2, PAIRS):
                    wait(dve, dve_h, t + 3)
                    fence(2)
                    nc.vector.bn_stats(stats[:], h_rows).then_inc(dve_st, 1)
                    wait(dve, dve_st, t + 3)
                    fence(3)
                    nc.vector.bn_aggr(moments[:], stats[:]).then_inc(dve_mom, 1)
                    add_eps(t + 2, moments, var_eps, dve_mom, dve_eps, pool_rstd)

            def stored(u, j):
                if isinstance(u, int):
                    return (u // 2 + 1) * 16 if u >= 0 else 0
                return (u - (1 - j)) * 8 + 16

            dve.wait_ge(s_w, 16 * 2)
            dve.wait_ge(act_whi, 1)
            nc.vector.tensor_tensor(w_tok_parts[1][:], w_tok[:], w_tok_parts[0][:].bitcast(F32),
                                    ALU.subtract).then_inc(dve_wlo, 1)
            dve.wait_ge(act_whi, 2)
            nc.vector.tensor_tensor(w_qkv_parts[1][:], w_qkv[:], w_qkv_parts[0][:].bitcast(F32),
                                    ALU.subtract).then_inc(dve_wlo, 1)
            run_steps(dve, step, *LOOP)

        @block.gpsimd
        def _(pool):
            for tile in (v_blocks, probs[0], probs[1]):
                nc.gpsimd.memset(tile[:], 0.0).then_inc(s_zero, 1)
            for tile in patch_parts[0] + patch_parts[1]:
                nc.gpsimd.memset(tile[:].bitcast(F32), 0.0).then_inc(s_zero, 1)
            nc.gpsimd.memset(minus_half[:], -0.5).then_inc(s_zero, 1)
            pool.wait_ge(s_zero, N_ZERO)
            pool.wait_ge(s_w, 16 * 2)

            def patches_low(u, j):
                wait(pool, act_phi, u + 1)
                wait(pool, pe_h, u - 1)
                cols = [[P, KC], [TP, IMGS], [1, T]]
                nc.gpsimd.tensor_tensor(view(patch_parts[j][1], 0, P, 0, cols),
                                        view(patches[j], 0, P, 0, [[PATCH_COLS, KC], [T, IMGS], [1, T]]),
                                        view(patch_parts[j][0], 0, P, 0, cols, F32), ALU.subtract).then_inc(pool_plo, 1)

            def inverse_std(u, ve, rs, s_eps, s_rstd, s_used):
                wait(pool, s_eps, u + 1)
                wait(pool, s_used, u)
                nc.gpsimd.tensor_tensor(rs[:], ve[:], minus_half[:], ALU.pow).then_inc(s_rstd, 1)

            def step(t, j):
                if exists(t, PAIRS):
                    wait(pool, dve_xn, t + 1)
                    h_rows = h_all[:, bass.ds(t * D, D)]
                    nc.gpsimd.tensor_tensor(h_rows, h_rows, b_proj[:], ALU.add).then_inc(pool_bias, 1)
                if exists(t - 3, PAIRS):
                    inverse_std(t - 3, var_eps2, rstd2, dve_eps2, pool_rstd2, dve_xn2)
                if exists(t + 1, PAIRS):
                    inverse_std(t + 1, var_eps, rstd, dve_eps, pool_rstd, dve_xn)
                if exists(t + 3, PAIRS) and not (isinstance(t, int) and t < -1):
                    patches_low(t + 3, 1 - j)
                if exists(t, PAIRS):
                    wait(pool, act_qkT, t + 1)
                    wait(pool, pe_s, 2 * t)
                    for c in range(DC):
                        nc.gpsimd.tensor_tensor(
                            view(k_blocks, 0, P, c * IMGS * SC, [[SC, IMGS], [T, HC], [1, T]]),
                            view(qkT, 0, P, (DC + c) * P, [[TP, IMGS], [0, HC], [1, T]]),
                            view(consts, 0, P, C_HEAD, [[0, IMGS], [1, HC], [0, T]]),
                            ALU.mult).then_inc(pool_kb, 1)
                if exists(t - 1, PAIRS):
                    wait(pool, dve_inv, t)
                    for c in range(DC):
                        pr = view(probs[1 - j], 0, P, c * HC * TP, [[TP, HC], [1, T]])
                        nc.gpsimd.tensor_tensor(pr, pr, view(row_inv, 0, P, c * HC, [[1, HC], [0, T]]),
                                                ALU.mult).then_inc(pool_norm, 1)

            patches_low(0, 0)
            patches_low(1, 1)
            pool.wait_ge(s_wqkv, 16 * 3)
            run_steps(pool, step, -2, 6, 28, PAIRS + 3)


def build_routing(nc, io, logits, consts, expert_weights, chosen_gate, slot_rows, slot_angles):
    with ExitStack() as ctx:
        def sb(name, cols, rows=P):
            return ctx.enter_context(nc.sbuf_tensor(name, [rows, cols], F32))

        def sem(name):
            return ctx.enter_context(nc.semaphore(name))

        HALVES = 2
        HALF = PAIRS // HALVES
        SETS = HALVES * IMGS
        RING = 4
        PARTS = 4
        QC = QUAD * E * PS
        gates = sb("gates", PAIRS * E)
        chosen = sb("chosen", PAIRS * E * PS)
        gate_rows = sb("gate_rows", SETS * TP)
        code_rows = sb("code_rows", SETS * TP)
        code_cols = sb("code_cols", PAIRS * E)
        top8 = sb("top8", SETS * 8)
        above = sb("above", SETS * T)
        ties = sb("ties", SETS * T)
        tie_rank = sb("tie_rank", SETS * T)
        taken = sb("taken", SETS * T)
        order = sb("order", SETS * T)
        room = sb("room", SETS)
        zeros = sb("zeros", T)
        rows = [sb(f"rows{j}", QUAD * D) for j in range(RING)]
        p_rows = ctx.enter_context(nc.psum_tensor("p_rows", [P, 512], F32))
        p_cols = ctx.enter_context(nc.psum_tensor("p_cols", [P, 512], F32))
        banks = [[ctx.enter_context(nc.psum_tensor(f"p_g{j}{c}", [P, 512], F32)) for c in range(DC + 1)]
                 for j in range(2)]
        r_exp, r_one, r_gate, r_rowsT, r_rows, r_zero, r_codeT, r_code, r_cols, r_clear, r_chosen, r_sel = (
            sem(n) for n in ("r_exp", "r_one", "r_gate", "r_rowsT", "r_rows", "r_zero", "r_codeT", "r_code",
                             "r_cols", "r_clear", "r_chosen", "r_sel"))
        g_in = [sem(f"g_in{j}") for j in range(RING)]
        g_mm, g_act, g_dve = sem("g_mm"), sem("g_act"), sem("g_dve")
        block = ctx.enter_context(nc.Block())

        @block.sync
        def _(sp):
            def load(q, j):
                wait(sp, g_mm, q - RING + 1)
                sp.dma_start(rows[j][:].rearrange("p (q n) -> p q n", q=QUAD),
                             io["xn2_dram"][bass.ds(q * QUAD, QUAD)].rearrange("q p n -> p q n")
                             ).then_inc(g_in[j], 16)

            for q in range(RING):
                load(q, q)
            for e in range(2):
                load_expert_weights(sp, io, expert_weights, e)
            for q in range(RING, NQ):
                load(q, q % RING)

        @block.tensor
        def _(pe):
            ident = consts[:, C_ID:C_ID + P]
            pe.wait_ge(r_gate, 1)
            for h in range(HALVES):
                last = nc.tensor.transpose(p_rows[:, h * P:(h + 1) * P],
                                           gates[:, h * HALF * E:(h + 1) * HALF * E], ident)
            last.then_inc(r_rowsT, 1)
            pe.wait_ge(r_code, 1)
            for h in range(HALVES):
                last = nc.tensor.transpose(p_cols[:, h * P:(h + 1) * P], code_rows[:, h * P:(h + 1) * P], ident)
            last.then_inc(r_codeT, 1)

            def gather(q, k, first):
                pe.wait_ge(g_in[k], 16 if first else 32)
                pe.wait_ge(r_chosen, IMGS * (k // 2 + (1 if first else 1 + PARTS // 2)))
                wait(pe, g_act, q - 1)
                wait(pe, g_dve, (q - 1) * 2)
                for n in range(QUAD):
                    for c in range(DC):
                        nc.tensor.matmul(banks[k % 2][c][:, n * E * PS:(n + 1) * E * PS],
                                         rows[k][:, n * D + c * P:n * D + (c + 1) * P],
                                         chosen[:, bass.ds(q * QC + n * E * PS, E * PS)], start=True, stop=True)
                nc.tensor.matmul(banks[k % 2][DC][:, 0:QC], consts[:, C_ROT:C_ROT + P],
                                 chosen[:, bass.ds(q * QC, QC)], start=True, stop=True).then_inc(g_mm, 1)

            for q in range(RING):
                gather(q, q, True)
            for q in range(RING, NQ):
                gather(q, q % RING, False)

        def spread(copy, dst, base, src, q):
            return copy(view(dst, 0, P, q * (QUAD * PS) + base, [[PS, QUAD], [NS, E], [1, PS]]),
                        view(src, 0, P, 0, [[E * PS, QUAD], [PS, E], [1, PS]]))

        @block.scalar
        def _(act):
            nc.scalar.activation(gates[:], logits[:], ACT.Exp, scale=-1.0).then_inc(r_exp, 1)
            with act.Fori(0, NQ // 2) as i:
                for j in range(2):
                    q = i * 2 + j
                    act.wait_ge(g_mm, q + 1)
                    spread(nc.scalar.copy, slot_rows, 0, banks[j][0], q).then_inc(g_act, 1)

        @block.vector
        def _(dve):
            dve.wait_ge(r_exp, 1)
            nc.vector.tensor_scalar(gates[:], gates[:], 1.0, None, ALU.add).then_inc(r_one, 1)
            dve.wait_ge(r_one, 1)
            nc.vector.reciprocal(gates[:], gates[:]).then_inc(r_gate, 1)
            dve.wait_ge(r_rowsT, 1)
            nc.vector.tensor_copy(gate_rows[:], p_rows[:, 0:SETS * TP]).then_inc(r_rows, 1)
            dve.wait_ge(r_rows, 1)
            dve.wait_ge(r_zero, 2)
            done = 0

            def settle(*ops):
                nonlocal done
                for op in ops:
                    op.then_inc(r_sel, 1)
                done += len(ops)
                dve.wait_ge(r_sel, done)

            def every(tile, pitch=T):
                return view(tile, 0, P, 0, [[pitch, SETS], [1, T]])

            def a_set(tile, k, pitch=T):
                return tile[:, k * pitch:k * pitch + T]

            def per_set(tile, off, pitch):
                return view(tile, 0, P, off, [[pitch, SETS], [0, T]])

            cut = per_set(top8, SLOTS - 1, 8)
            settle(*[nc.vector.max(top8[:, k * 8:(k + 1) * 8], a_set(gate_rows, k, TP)) for k in range(SETS)])
            settle(nc.vector.tensor_tensor(every(above), every(gate_rows, TP), cut, ALU.is_gt),
                   nc.vector.tensor_tensor(every(ties), every(gate_rows, TP), cut, ALU.is_equal))
            settle(nc.vector.tensor_reduce(room[:], every(above), AX, ALU.add),
                   *[nc.vector.tensor_tensor_scan(a_set(tie_rank, k), a_set(ties, k), zeros[:], 0.0,
                                                  ALU.add, ALU.add) for k in range(SETS)])
            settle(nc.vector.tensor_scalar(room[:], room[:], -1.0, float(SLOTS), ALU.mult, ALU.add))
            settle(nc.vector.tensor_tensor(every(taken), every(tie_rank), per_set(room, 0, 1), ALU.is_le))
            settle(nc.vector.tensor_tensor(every(taken), every(taken), every(ties), ALU.mult))
            settle(nc.vector.tensor_tensor(every(taken), every(taken), every(above), ALU.add))
            settle(*[nc.vector.tensor_tensor_scan(a_set(order, k), a_set(taken, k), zeros[:], 0.0,
                                                  ALU.add, ALU.add) for k in range(SETS)])
            nc.vector.tensor_tensor(every(code_rows, TP), every(order), every(taken), ALU.mult).then_inc(r_code, 1)
            dve.wait_ge(r_codeT, 1)
            nc.vector.tensor_copy(code_cols[:], p_cols[:, 0:PAIRS * E]).then_inc(r_cols, 1)
            dve.wait_ge(r_cols, 1)
            dve.wait_ge(r_clear, 1)
            n = PAIRS * E // PARTS
            for part in range(PARTS):
                for b in range(IMGS):
                    nc.vector.tensor_tensor(
                        view(chosen, b * TP, TP, part * n * PS + b * SLOTS, [[PS, n], [1, SLOTS]]),
                        view(code_cols, b * TP, TP, part * n, [[1, n], [0, SLOTS]]),
                        view(consts, b * TP, TP, C_SLOT, [[0, n], [1, SLOTS]]),
                        ALU.is_equal).then_inc(r_chosen, 1)
            with dve.Fori(0, NQ // 2) as i:
                for j in range(2):
                    q = i * 2 + j
                    dve.wait_ge(g_mm, q + 1)
                    spread(nc.vector.tensor_copy, slot_rows, E * NS, banks[j][1], q).then_inc(g_dve, 1)
                    spread(nc.vector.tensor_copy, slot_angles, 0, banks[j][2], q).then_inc(g_dve, 1)

        @block.gpsimd
        def _(pool):
            nc.gpsimd.memset(code_rows[:], 0.0).then_inc(r_zero, 1)
            nc.gpsimd.memset(zeros[:], 0.0).then_inc(r_zero, 1)
            nc.gpsimd.memset(chosen[:], 0.0).then_inc(r_clear, 1)
            pool.wait_ge(r_chosen, IMGS * PARTS)
            nc.gpsimd.tensor_tensor(view(chosen_gate, 0, P, 0, [[PS, PAIRS * E], [1, PS]]),
                                    view(chosen, 0, P, 0, [[PS, PAIRS * E], [1, PS]]),
                                    view(gates, 0, P, 0, [[1, PAIRS * E], [0, PS]]), ALU.mult)


class ExpertWeights:

    def __init__(self, nc, ctx):
        def sb(name, cols):
            return ctx.enter_context(nc.sbuf_tensor(name, [P, cols], F32))

        self.qkv = [sb(f"w_e{j}", DC * 3 * HP) for j in range(2)]
        self.out = [sb(f"wo_e{j}", D) for j in range(4)]
        self.qkv_in = [ctx.enter_context(nc.semaphore(f"e_qkv{j}")) for j in range(2)]
        self.out_in = [ctx.enter_context(nc.semaphore(f"e_out{j}")) for j in range(4)]


def load_expert_weights(sp, io, weights, e):
    sp.dma_start(weights.qkv[e % 2][:].rearrange("p (c n) -> p c n", c=DC),
                 io["L0_ffn_Wqkv"][e].rearrange("(c p) n -> p c n", p=P)).then_inc(weights.qkv_in[e % 2], 16)
    sp.dma_start(weights.out[e % 4][:], io["L0_ffn_Wo"][e]).then_inc(weights.out_in[e % 4], 16)


def build_experts(nc, io, consts, weights, slot_rows, slot_angles, slot_out):
    with ExitStack() as ctx:
        def sb(name, cols, rows=P):
            return ctx.enter_context(nc.sbuf_tensor(name, [rows, cols], F32))

        def sem(name):
            return ctx.enter_context(nc.semaphore(name))

        x_e = [sb(f"x_e{j}", DC * NS) for j in range(2)]
        w_e, wo_e = weights.qkv, weights.out
        turned = sb("turned", 2 * NS)
        straight = sb("straight", 2 * NS, 2 * ROT)
        qk = [sb(f"qk{j}", 2 * NS) for j in range(2)]
        v = [sb(f"v{j}", NG * HP, GS) for j in range(4)]
        s_e = sb("s_e", NG * GS, GS)
        a_e = sb("a_e", NG * GS, GS)
        aT = sb("aT", NG * GS, GS)
        avT = sb("avT", NS)
        mx = sb("mx", NG, GS)
        sm = sb("sm", NG, GS)
        inv = sb("inv", NG, GS)
        p_qk = ctx.enter_context(nc.psum_tensor("p_qke", [P, 1024], F32))
        p_v, p_s, p_aT, p_av = (ctx.enter_context(nc.psum_tensor(n, [P, 512], F32))
                                for n in ("p_ve", "p_se", "p_aTe", "p_ave"))
        p_o = ctx.enter_context(nc.psum_tensor("p_oe", [P, 1024], F32))
        e_in = [sem(f"e_in{j}") for j in range(2)]
        (m_qk, m_v, m_s, m_aT, m_av, m_o) = (sem(n) for n in ("m_qk", "m_v", "m_s", "m_aT", "m_av", "m_o"))
        (a_rest, a_v, a_exp, a_aT, a_av, a_o) = (sem(n) for n in ("a_rest", "a_v", "a_exp", "a_aT", "a_av", "a_o"))
        (d_turn, d_rope, d_mask, d_max, d_shift, d_sum, d_inv, d_norm, d_o) = (
            sem(n) for n in ("d_turn", "d_rope", "d_mask", "d_max", "d_shift", "d_sum", "d_inv", "d_norm", "d_o"))
        g_s, e_first = sem("g_s"), sem("e_first")
        block = ctx.enter_context(nc.Block())

        def run(eng, step):
            for t in range(E + 2):
                step(t, t % 2)

        @block.sync
        def _(sp):
            for e in range(E):
                j = e % 2
                if e == 0:
                    continue
                wait(sp, m_v, e - 1)
                sp.dma_start(x_e[j][:].rearrange("p (c n) -> p c n", c=DC),
                             view(slot_rows, 0, P, e * NS, [[E * NS, DC], [1, NS]])).then_inc(e_in[j], 16)
                if e >= 2:
                    wait(sp, m_o, e - 3)
                    load_expert_weights(sp, io, weights, e)

        @block.tensor
        def _(pe):
            ident = consts[:, C_ID:C_ID + P]

            def transpose_attention(u):
                wait(pe, d_norm, u + 1)
                wait(pe, a_aT, u)
                for g in range(NG):
                    last = nc.tensor.transpose(p_aT[0:GS, g * GS:(g + 1) * GS],
                                               a_e[:, g * GS:(g + 1) * GS], ident[0:GS, 0:GS])
                last.then_inc(m_aT, 1)

            def queries_keys(u, j):
                if u == 0:
                    pe.wait_ge(e_first, 2)
                else:
                    pe.wait_ge(e_in[j], 16 * ((u + j) // 2))
                wait(pe, weights.qkv_in[j], 16 * (u // 2 + 1))
                wait(pe, a_rest, u)
                wait(pe, d_turn, 2 * u)
                wait(pe, d_rope, 2 * u)
                for k in range(2):
                    for c in range(DC):
                        last = nc.tensor.matmul(p_qk[:, k * 512:k * 512 + NS],
                                                w_e[j][:, c * 3 * HP + k * HP:c * 3 * HP + (k + 1) * HP],
                                                x_e[j][:, c * NS:(c + 1) * NS], start=c == 0, stop=c == DC - 1)
                last.then_inc(m_qk, 1)

            def values(u, j):
                wait(pe, a_v, u)
                for g in range(NG):
                    for c in range(DC):
                        last = nc.tensor.matmul(p_v[0:GS, g * HP:(g + 1) * HP],
                                                x_e[j][:, c * NS + g * GS:c * NS + (g + 1) * GS],
                                                w_e[j][:, c * 3 * HP + 2 * HP:(c + 1) * 3 * HP],
                                                start=c == 0, stop=c == DC - 1)
                last.then_inc(m_v, 1)

            def scores(u, j):
                wait(pe, g_s, u + 1)
                wait(pe, a_rest, u + 1)
                wait(pe, d_mask, u)
                for g in range(NG):
                    last = nc.tensor.matmul(p_s[0:GS, g * GS:(g + 1) * GS], qk[j][:, g * GS:(g + 1) * GS],
                                            qk[j][:, NS + g * GS:NS + (g + 1) * GS], start=True, stop=True)
                last.then_inc(m_s, 1)

            def attend(u):
                wait(pe, a_aT, u + 1)
                wait(pe, a_v, u + 1)
                wait(pe, a_av, u)
                for g in range(NG):
                    last = nc.tensor.matmul(p_av[:, g * GS:(g + 1) * GS], v[u % 4][:, g * HP:(g + 1) * HP],
                                            aT[:, g * GS:(g + 1) * GS], start=True, stop=True)
                last.then_inc(m_av, 1)

            def project(u):
                wait(pe, a_av, u + 1)
                wait(pe, weights.out_in[u % 4], 16 * (u // 4 + 1))
                wait(pe, a_o, u)
                wait(pe, d_o, u)
                for c in range(DC):
                    last = nc.tensor.matmul(p_o[:, c * 512:c * 512 + NS], wo_e[u % 4][:, c * P:(c + 1) * P],
                                            avT[:], start=True, stop=True)
                last.then_inc(m_o, 1)

            def step(t, j):
                if exists(t, E):
                    queries_keys(t, j)
                if exists(t - 2, E):
                    transpose_attention(t - 2)
                if exists(t - 1, E):
                    scores(t - 1, 1 - j)
                if exists(t - 2, E):
                    attend(t - 2)
                if exists(t, E):
                    values(t, j)
                if exists(t - 2, E):
                    project(t - 2)

            run(pe, step)

        def leave(copy, u, c):
            return copy(view(slot_out, 0, P, (c * E + u) * PS, [[DC * E * PS, PAIRS], [1, PS]]),
                        view(p_o, 0, P, c * 512, [[PS, PAIRS], [1, PS]]))

        @block.scalar
        def _(act):
            def step(t, j):
                if exists(t, E):
                    wait(act, m_qk, t + 1)
                    wait(act, m_s, t - 1)
                    nc.scalar.copy(view(qk[j], 2 * ROT, P - 2 * ROT, 0, [[NS, 2], [1, NS]]),
                                   view(p_qk, 2 * ROT, P - 2 * ROT, 0, [[512, 2], [1, NS]])).then_inc(a_rest, 1)
                if exists(t - 2, E):
                    wait(act, m_aT, t - 1)
                    nc.scalar.copy(aT[:], p_aT[0:GS, 0:NG * GS]).then_inc(a_aT, 1)
                if exists(t - 2, E):
                    wait(act, m_av, t - 1)
                    nc.scalar.copy(avT[:], p_av[:, 0:NS]).then_inc(a_av, 1)
                if exists(t - 1, E):
                    wait(act, d_shift, t)
                    wait(act, m_aT, t - 1)
                    nc.scalar.activation(a_e[:], s_e[:], ACT.Exp, scale=float(HP) ** -0.5).then_inc(a_exp, 1)
                if exists(t, E):
                    wait(act, m_v, t + 1)
                    nc.scalar.copy(v[t % 4][:], p_v[0:GS, :]).then_inc(a_v, 1)
                if exists(t - 2, E):
                    wait(act, m_o, t - 1)
                    leave(nc.scalar.copy, t - 2, 0).then_inc(a_o, 1)

            nc.scalar.copy(x_e[0][:, 0:NS], slot_rows[:, 0:NS]).then_inc(e_first, 1)
            run(act, step)

        @block.vector
        def _(dve):
            def step(t, j):
                if exists(t, E):
                    wait(dve, m_qk, t + 1)
                    wait(dve, g_s, t)
                    for lo, hi in ((0, ROT), (ROT, 0)):
                        nc.vector.tensor_tensor(view(turned, lo, ROT, 0, [[NS, 2], [1, NS]]),
                                                view(p_qk, hi, ROT, 0, [[512, 2], [1, NS]]),
                                                view(slot_angles, 2 * ROT + lo, ROT, t * NS, [[0, 2], [1, NS]]),
                                                ALU.mult).then_inc(d_turn, 1)
                    nc.vector.tensor_tensor(view(straight, 0, 2 * ROT, 0, [[NS, 2], [1, NS]]),
                                            view(p_qk, 0, 2 * ROT, 0, [[512, 2], [1, NS]]),
                                            view(slot_angles, 0, 2 * ROT, t * NS, [[0, 2], [1, NS]]),
                                            ALU.mult).then_inc(d_rope, 2)
                if exists(t - 1, E):
                    u = t - 1
                    wait(dve, m_s, u + 1)
                    wait(dve, a_exp, u)
                    nc.vector.tensor_tensor(view(s_e, 0, GS, 0, [[GS, NG], [1, GS]]),
                                            view(p_s, 0, GS, 0, [[GS, NG], [1, GS]]),
                                            view(consts, 0, GS, C_MASKF, [[0, NG], [1, GS]]),
                                            ALU.add).then_inc(d_mask, 1)
                    wait(dve, d_mask, u + 1)
                    s3 = view(s_e, 0, GS, 0, [[GS, NG], [1, GS]])
                    nc.vector.tensor_reduce(mx[:], s3, AX, ALU.max).then_inc(d_max, 1)
                    wait(dve, d_max, u + 1)
                    nc.vector.tensor_tensor(s3, s3, view(mx, 0, GS, 0, [[1, NG], [0, GS]]),
                                            ALU.subtract).then_inc(d_shift, 1)
                if exists(t - 1, E):
                    u = t - 1
                    wait(dve, a_exp, u + 1)
                    a3 = view(a_e, 0, GS, 0, [[GS, NG], [1, GS]])
                    nc.vector.tensor_reduce(sm[:], a3, AX, ALU.add).then_inc(d_sum, 1)
                    wait(dve, d_sum, u + 1)
                    nc.vector.reciprocal(inv[:], sm[:]).then_inc(d_inv, 1)
                    wait(dve, d_inv, u + 1)
                    nc.vector.tensor_tensor(a3, a3, view(inv, 0, GS, 0, [[1, NG], [0, GS]]),
                                            ALU.mult).then_inc(d_norm, 1)
                if exists(t - 2, E):
                    wait(dve, m_o, t - 1)
                    leave(nc.vector.tensor_copy, t - 2, 1).then_inc(d_o, 1)

            nc.vector.tensor_copy(x_e[0][:, NS:2 * NS], slot_rows[:, E * NS:(E + 1) * NS]).then_inc(e_first, 1)
            run(dve, step)

        @block.gpsimd
        def _(pool):
            for t in range(E):
                wait(pool, d_turn, 2 * (t + 1))
                wait(pool, d_rope, 2 * (t + 1))
                wait(pool, m_s, t - 1)
                nc.gpsimd.tensor_tensor(qk[t % 2][0:2 * ROT, :], straight[:], turned[0:2 * ROT, :],
                                        ALU.add).then_inc(g_s, 1)


def build_scatter(nc, io, consts, h_all, slot_out, chosen_gate):
    with ExitStack() as ctx:
        def sb(name, cols, rows=P):
            return ctx.enter_context(nc.sbuf_tensor(name, [rows, cols], F32))

        def sem(name):
            return ctx.enter_context(nc.semaphore(name))

        ES = E * PS
        outs = [sb(f"outs{j}", QUAD * DC * ES) for j in range(2)]
        gts = [sb(f"gts{j}", QUAD * ES) for j in range(2)]
        back = [sb(f"back{j}", DC * P + P, ES) for j in range(2)]
        final = [sb(f"final{j}", QUAD * D) for j in range(2)]
        p_t = [ctx.enter_context(nc.psum_tensor(f"p_t{j}", [P, 512], F32)) for j in range(2)]
        p_f = [ctx.enter_context(nc.psum_tensor(f"p_f{j}", [P, 512], F32)) for j in range(2)]
        c_in = sem("c_in")
        c_out = [sem(f"c_out{j}") for j in range(2)]
        c_T, c_back, c_mm, c_fin = sem("c_T"), sem("c_back"), sem("c_mm"), sem("c_fin")
        block = ctx.enter_context(nc.Block())

        @block.sync
        def _(sp):
            def store(q, j):
                wait(sp, c_fin, (q + 1) * QUAD)
                for b in range(IMGS):
                    sp.dma_start(io["out"][bass.ds(q * QUAD, QUAD), b].rearrange("q t n -> t q n"),
                                 final[j][b * TP:b * TP + T, :].rearrange("t (q n) -> t q n", q=QUAD)
                                 ).then_inc(c_out[j], 16)

            with sp.Fori(0, NQ // 2) as i:
                for j in range(2):
                    store(i * 2 + j, j)
            for j in range(2):
                sp.wait_ge(c_out[j], 16 * IMGS * NQ // 2)

        def quads(eng, body):
            for q in range(2):
                for k in range(QUAD):
                    body(q, q, k, q * QUAD + k)
            with eng.Fori(1, NQ // 2) as i:
                for j in range(2):
                    for k in range(QUAD):
                        q = i * 2 + j
                        body(q, j, k, q * QUAD + k)

        @block.tensor
        def _(pe):
            ident = consts[:, C_ID:C_ID + P]

            def scatter(u, k):
                wait(pe, c_back, u + 1)
                wait(pe, c_fin, u - 1)
                nc.tensor.matmul(p_f[k % 2][:, 0:D], back[k % 2][:, DC * P:], back[k % 2][:, 0:D],
                                 start=True, stop=True).then_inc(c_mm, 1)

            def body(q, j, k, u):
                if k == 0:
                    wait(pe, c_in, (q + 1) * 2)
                wait(pe, c_back, u - 1)
                for c in range(DC):
                    nc.tensor.transpose(p_t[k % 2][0:ES, c * P:(c + 1) * P],
                                        outs[j][:, (k * DC + c) * ES:(k * DC + c + 1) * ES], ident)
                nc.tensor.transpose(p_t[k % 2][0:ES, DC * P:DC * P + P], gts[j][:, k * ES:(k + 1) * ES],
                                    ident).then_inc(c_T, 1)
                if not (isinstance(u, int) and u == 0):
                    scatter(u - 1, k - 1)

            quads(pe, body)
            scatter(PAIRS - 1, QUAD - 1)

        @block.scalar
        def _(act):
            def body(q, j, k, u):
                wait(act, c_T, u + 1)
                wait(act, c_mm, u - 1)
                nc.scalar.copy(back[k % 2][:], p_t[k % 2][0:ES, 0:DC * P + P]).then_inc(c_back, 1)

            quads(act, body)

        @block.vector
        def _(dve):
            def fetch(q, j):
                wait(dve, c_T, (q - 1) * QUAD)
                nc.vector.tensor_copy(outs[j][:], slot_out[:, bass.ds(q * (QUAD * DC * ES), QUAD * DC * ES)]
                                      ).then_inc(c_in, 1)
                nc.vector.tensor_copy(gts[j][:], chosen_gate[:, bass.ds(q * (QUAD * ES), QUAD * ES)]
                                      ).then_inc(c_in, 1)

            def body(q, j, k, u, ahead=True):
                if k == 1 and ahead:
                    fetch(q + 1, 1 - j)
                wait(dve, c_mm, u + 1)
                if k == 0:
                    wait(dve, c_out[j], (q - j) * 16)
                nc.vector.tensor_tensor(final[j][:, k * D:(k + 1) * D], p_f[k % 2][:, 0:D],
                                        h_all[:, bass.ds(u * D, D)], ALU.add).then_inc(c_fin, 1)

            fetch(0, 0)
            for q in range(2):
                for k in range(QUAD):
                    body(q, q, k, q * QUAD + k)
            with dve.Fori(1, NQ // 2 - 1) as i:
                for j in range(2):
                    for k in range(QUAD):
                        q = i * 2 + j
                        body(q, j, k, q * QUAD + k)
            for q in range(NQ - 2, NQ):
                for k in range(QUAD):
                    body(q, q % 2, k, q * QUAD + k, ahead=q < NQ - 1)


def build(nc, io):
    with ExitStack() as ctx:
        def sb(name, cols):
            return ctx.enter_context(nc.sbuf_tensor(name, [P, cols], F32))

        consts = sb("consts", C_END)
        h_all = sb("h_all", PAIRS * D)
        logits = sb("logits", PAIRS * E)
        build_attention(nc, io, h_all, logits, consts)
        chosen_gate = sb("chosen_gate", PAIRS * E * PS)
        slot_out = sb("slot_out", PAIRS * DC * E * PS)
        slot_rows = sb("slot_rows", DC * E * NS)
        slot_angles = sb("slot_angles", E * NS)
        weights = ExpertWeights(nc, ctx)
        build_routing(nc, io, logits, consts, weights, chosen_gate, slot_rows, slot_angles)
        build_experts(nc, io, consts, weights, slot_rows, slot_angles, slot_out)
        build_scatter(nc, io, consts, h_all, slot_out, chosen_gate)


def constants():
    import numpy as np
    c = np.zeros((P, C_END), np.float32)
    row = np.arange(P)
    tok = (row % TP).astype(np.float32)
    c[:, C_ID:C_ID + P] = np.eye(P)
    inv = np.float32(1.0) / np.power(np.float32(10000.0), np.arange(0, HD, 2, dtype=np.float32) / np.float32(HD))
    ang = tok[:, None] * inv.astype(np.float32)[None]
    c[:, C_COS:C_COS + HD] = np.tile(np.cos(ang), 2)
    c[:, C_SIN:C_SIN + HD] = np.concatenate([-np.sin(ang), np.sin(ang)], 1)
    c[:, C_CAUSAL:C_CAUSAL + T] = np.where(np.arange(T)[None] <= (row % TP)[:, None], 0.0, NEG)
    c[:, C_HEAD:C_HEAD + HC] = (row // HD)[:, None] == np.arange(HC)[None]
    inv = np.float32(1.0) / np.power(np.float32(10000.0),
                                     np.arange(ROT, dtype=np.float32) * np.float32(2.0) / np.float32(2 * ROT))
    ang = tok[:, None] * inv.astype(np.float32)[None]
    c[:, C_ROT:C_ROT + P] = np.concatenate([np.cos(ang), np.cos(ang), -np.sin(ang), np.sin(ang)], 1)
    q, k = np.arange(P)[:, None], np.arange(GS)[None]
    c[:, C_MASKF:C_MASKF + GS] = np.where((q // SLOTS == k // SLOTS) & (k <= q), 0.0, NEG)
    c[:, C_SLOT:C_SLOT + SLOTS] = np.arange(1, SLOTS + 1)
    return c


def kernel(x, L0_tok_W, L0_tok_b, L0_attn_w_qkv, L0_attn_w_proj, L0_attn_b_proj, L0_ffn_Wr, L0_ffn_Wqkv, L0_ffn_Wo):
    import numpy as np
    import concourse.bacc as bacc
    from concourse.bass_utils import run_bass_kernel_spmd

    nc = bacc.Bacc("TRN2", target_bir_lowering=False, num_devices=1)
    xs = np.asarray(x).reshape(PAIRS, IMGS, 3, 7, 16, 7, 16).transpose(0, 2, 4, 6, 1, 3, 5)
    xs = xs.reshape(PAIRS, KC, P, PATCH_COLS).transpose(0, 2, 1, 3).reshape(PAIRS, P, KC * PATCH_COLS)
    router = np.asarray(L0_ffn_Wr).T.reshape(DC, P, E).transpose(1, 0, 2).reshape(P, DC * E)
    arrays = {"patchesT": xs, "routerT": router, "consts": constants(), "L0_tok_W": L0_tok_W, "L0_tok_b": L0_tok_b,
              "L0_attn_w_qkv": L0_attn_w_qkv, "L0_attn_w_proj": L0_attn_w_proj, "L0_attn_b_proj": L0_attn_b_proj,
              "L0_ffn_Wqkv": L0_ffn_Wqkv, "L0_ffn_Wo": L0_ffn_Wo}
    arrays = {n: np.ascontiguousarray(a) for n, a in arrays.items()}
    io = {n: nc.dram_tensor("in_" + n, a.shape, mybir.dt.from_np(a.dtype), kind="ExternalInput").ap()
          for n, a in arrays.items()}
    io["xn2_dram"] = nc.dram_tensor("xn2_dram", (PAIRS, P, D), F32, kind="Internal").ap()
    out = nc.dram_tensor("out_rows", (PAIRS, IMGS, T, D), F32, kind="ExternalOutput").ap()
    io["out"] = out
    build(nc, io)
    r = run_bass_kernel_spmd(nc, [{"in_" + n: a for n, a in arrays.items()}], core_ids=[0])
    return r.results[0]["out_rows"].reshape(PAIRS * IMGS, T, D)
```

```python
from contextlib import ExitStack

import concourse.bass as bass
from concourse import mybir

F32 = mybir.dt.float32
F32R = mybir.dt.float32r
ALU = mybir.AluOpType
ACT = mybir.ActivationFunctionType
AX = mybir.AxisListType.X

P = 128
T = 49
TP = 64
IMGS = 2
PAIRS = 32
D = 256
DC = D // P
KC = 768 // P
PATCH_COLS = IMGS * T
HEADS, HD = 16, 16
HC = HEADS // 2
SC = HC * T
EPS = 1e-5
E, HP, SLOTS = 8, 128, 6
ROT = 32
PS = IMGS * SLOTS
NS = PAIRS * PS
GROUP = 8
GS = GROUP * PS
NG = PAIRS // GROUP
QUAD = 4
NQ = PAIRS // QUAD
NEG = -1.0e30

C_ID = 0
C_COS = C_ID + P
C_SIN = C_COS + HD
C_CAUSAL = C_SIN + HD
C_HEAD = C_CAUSAL + T
C_ROT = C_HEAD + HC
C_MASKF = C_ROT + P
C_SLOT = C_MASKF + GS
C_END = C_SLOT + SLOTS


def view(tile, p0, n, off, dims, dtype=None):
    base = tile[p0:p0 + n, bass.ds(off, 1)] if not isinstance(off, int) else tile[p0:p0 + n, off:off + 1]
    if dtype is not None:
        base = base.bitcast(dtype)
    return bass.AP(tensor=base.tensor, offset=base.offset, ap=[list(base.ap[0])] + [list(d) for d in dims])


def wait(eng, sem, value):
    if isinstance(value, int) and value <= 0:
        return
    eng.wait_ge(sem, value)


def pair_loads(u, j):
    return (u // 2 + 1) * 16 if isinstance(u, int) else (u - j) * 8 + 16


def three_passes(w, x):
    return ((w[0], x[0]), (w[1], x[0]), (w[0], x[1]))


def keep_clock_up(nc, consts, bank, count):
    ident = consts[:, C_ID:C_ID + P]
    for _ in range(count):
        nc.tensor.matmul(bank[:, 0:P], ident, ident, start=True, stop=True)


def exists(u, n):
    return not isinstance(u, int) or 0 <= u < n


UNROLL = 4


def run_steps(eng, step, first, loop_from, loop_to, last):
    for t in range(first, loop_from):
        step(t, t % 2)
    with eng.Fori(0, (loop_to - loop_from) // UNROLL) as i:
        for j in range(UNROLL):
            step(i * UNROLL + (loop_from + j), j % 2)
    for t in range(loop_to, last):
        step(t, t % 2)


def build_attention(nc, io, h_all, logits, consts):
    with ExitStack() as ctx:
        def sb(name, cols, dtype=F32):
            return ctx.enter_context(nc.sbuf_tensor(name, [P, cols], dtype))

        def parts(name, cols):
            return sb(name + "_hi", cols, F32R), sb(name + "_lo", cols, F32R)

        def sem(name):
            return ctx.enter_context(nc.semaphore(name))

        w_tok = sb("w_tok", KC * D)
        w_tok_parts = parts("w_tok", KC * D)
        w_qkv_parts = parts("w_qkv", DC * 3 * D)
        patch_parts = [parts(f"patch{j}", KC * P) for j in range(2)]
        xnT_parts = parts("xnT", D)
        w_qkv = sb("w_qkv", DC * 3 * D)
        w_proj = sb("w_proj", DC * D)
        w_router = sb("w_router", DC * E)
        b_tok = sb("b_tok", D)
        b_proj = sb("b_proj", D)
        patches = [sb(f"patches{j}", KC * PATCH_COLS) for j in range(2)]
        xn = [sb(f"xn{j}", D) for j in range(2)]
        xn2 = [sb(f"xn2_{j}", D) for j in range(2)]
        xn2T = sb("xn2T", D)
        qk_cos = sb("qk_cos", 2 * D)
        qk_sin = sb("qk_sin", 2 * D)
        qk_rot = sb("qk_rot", 2 * D)
        qkT = sb("qkT", 4 * P)
        k_blocks = sb("k_blocks", DC * IMGS * SC)
        scores = sb("scores", HEADS * T)
        probs = [sb(f"probs{j}", HEADS * TP) for j in range(2)]
        probsT = sb("probsT", 2 * 4 * P)
        v_rows = [sb(f"v_rows{j}", D) for j in range(2)]
        v_blocks = sb("v_blocks", IMGS * HC * 2 * HD)
        attnT = sb("attnT", D)
        row_max = sb("row_max", HEADS)
        row_sum = sb("row_sum", HEADS)
        row_inv = sb("row_inv", HEADS)
        stats = sb("stats", 6)
        stats2 = sb("stats2", 6)
        moments = sb("moments", 2)
        moments2 = sb("moments2", 2)
        var_eps = sb("var_eps", 1)
        var_eps2 = sb("var_eps2", 1)
        rstd = sb("rstd", 1)
        rstd2 = sb("rstd2", 1)
        minus_half = sb("minus_half", 1)
        fences = sb("fences", 4)

        def bank(name):
            return ctx.enter_context(nc.psum_tensor(name, [P, 512], F32))

        p_h = bank("p_h")
        p_xT = bank("p_xT")
        p_qk = bank("p_qk")
        p_v = bank("p_v")
        p_mix = bank("p_mix")
        p_s = ctx.enter_context(nc.psum_tensor("p_s", [P, 1024], F32))
        p_pT = bank("p_pT")

        W_CUTS = 2
        s_wtok = [sem(f"s_wtok{k}") for k in range(W_CUTS)]
        s_w, s_wq, s_wqkv = (sem(n) for n in ("s_w", "s_wq", "s_wqkv"))
        s_zero = sem("s_zero")
        s_clear = sem("s_clear")
        s_pat = [sem(f"s_pat{j}") for j in range(2)]
        s_store = [sem(f"s_store{j}") for j in range(2)]
        pe_h, pe_xT, pe_qk, pe_v, pe_qkT, pe_s, pe_pT, pe_av, pe_proj, pe_x2T, pe_lg = (
            sem(n) for n in ("pe_h", "pe_xT", "pe_qk", "pe_v", "pe_qkT", "pe_s", "pe_pT", "pe_av", "pe_proj",
                             "pe_x2T", "pe_lg"))
        act_whi, act_phi, dve_wlo, dve_xlo, pool_plo, pool_bias = (
            sem(n) for n in ("act_whi", "act_phi", "dve_wlo", "dve_xlo", "pool_plo", "pool_bias"))
        act_xT, act_exp, act_v, act_pT, act_av, act_x2T, act_qkT, act_lg, act_vb = (
            sem(n) for n in ("act_xT", "act_exp", "act_v", "act_pT", "act_av", "act_x2T", "act_qkT", "act_lg",
                             "act_vb"))
        dve_mask, dve_max, dve_shift, dve_rope, dve_rot, dve_xn2, dve_xn, dve_sum, dve_inv = (
            sem(n) for n in ("dve_mask", "dve_max", "dve_shift", "dve_rope", "dve_rot", "dve_xn2", "dve_xn", "dve_sum",
                             "dve_inv"))
        dve_res, dve_st2, dve_mom2, dve_h, dve_st, dve_mom = (
            sem(n) for n in ("dve_res", "dve_st2", "dve_mom2", "dve_h", "dve_st", "dve_mom"))
        pool_kb, pool_norm, pool_rstd, pool_rstd2, dve_eps, dve_eps2 = (
            sem(n) for n in ("pool_kb", "pool_norm", "pool_rstd", "pool_rstd2", "dve_eps", "dve_eps2"))
        N_ZERO = 5

        def a_cut(tile, k):
            return tile[:, k * KC * D // W_CUTS:(k + 1) * KC * D // W_CUTS]

        LOOP = (-2, 6, 30, PAIRS + 3)
        block = ctx.enter_context(nc.Block())

        @block.sync
        def _(sp):
            def load_patches(u, j):
                wait(sp, pool_plo, u - 1)
                sp.dma_start(patches[j][:], io["patchesT"][u]).then_inc(s_pat[j], 16)

            load_patches(0, 0)
            for k in range(W_CUTS):
                n = KC // W_CUTS
                sp.dma_start(a_cut(w_tok, k).rearrange("p (c n) -> p c n", c=n),
                             io["L0_tok_W"][k * n * P:(k + 1) * n * P].rearrange("(c p) n -> p c n", p=P)
                             ).then_inc(s_wtok[k], 16)
            sp.dma_start(w_qkv[:].rearrange("p (c n) -> p c n", c=DC),
                         io["L0_attn_w_qkv"].rearrange("(c p) n -> p c n", p=P)).then_inc(s_wq, 16)
            sp.dma_start(b_tok[:], io["L0_tok_b"].partition_broadcast(P)).then_inc(s_w, 16)
            sp.dma_start(consts[:], io["consts"]).then_inc(s_w, 16)
            load_patches(1, 1)
            sp.dma_start(w_proj[:].rearrange("p (c n) -> p c n", c=DC),
                         io["L0_attn_w_proj"].rearrange("(c p) n -> p c n", p=P)).then_inc(s_wqkv, 16)
            sp.dma_start(b_proj[:], io["L0_attn_b_proj"].partition_broadcast(P)).then_inc(s_wqkv, 16)
            sp.dma_start(w_router[:], io["routerT"]).then_inc(s_wqkv, 16)

            def step(t, j):
                if exists(t - 3, PAIRS):
                    wait(sp, dve_xn2, t - 2)
                    sp.dma_start(io["xn2_dram"][t - 3], xn2[1 - j][:]).then_inc(s_store[1 - j], 16)
                if exists(t + 4, PAIRS):
                    load_patches(t + 4, j)

            run_steps(sp, step, -2, 6, 26, PAIRS + 3)
            for j in range(2):
                sp.wait_ge(s_store[j], 16 * PAIRS // 2)

        @block.tensor
        def _(pe):
            ident = consts[:, C_ID:C_ID + P]
            pe.wait_ge(s_zero, N_ZERO)

            def min_pair(n):
                return min(n, PAIRS) if isinstance(n, int) else n

            def embed(u, j):
                wait(pe, act_phi, u + 1)
                wait(pe, dve_h, u)
                wait(pe, dve_res, u - 4)
                for n, (w, x) in enumerate(three_passes(w_tok_parts, patch_parts[j])):
                    if n == 2:
                        wait(pe, pool_plo, u + 1)
                    for c in range(KC):
                        if isinstance(u, int) and u == 0 and n < 2 and c % (KC // W_CUTS) == 0:
                            pe.wait_ge((act_whi, dve_wlo)[n], c // (KC // W_CUTS) + 1)
                        last = nc.tensor.matmul(p_h[:, 0:D], x[:, c * P:(c + 1) * P], w[:, c * D:(c + 1) * D],
                                                start=n == 0 and c == 0, stop=n == 2 and c == KC - 1)
                last.then_inc(pe_h, 1)

            def transpose_rows(src, sem_done):
                for c in range(DC):
                    last = nc.tensor.transpose(p_xT[:, c * P:(c + 1) * P], src[:, c * P:(c + 1) * P], ident)
                last.then_inc(sem_done, 1)

            def first_rows(u, j):
                wait(pe, dve_xn, u + 1)
                wait(pe, act_x2T, u - 3)
                transpose_rows(xn[j], pe_xT)

            def qkv(u):
                wait(pe, act_xT, u + 1)
                wait(pe, dve_rope, 2 * u)
                for n, (w, x) in enumerate(three_passes(w_qkv_parts, xnT_parts)):
                    if n == 2:
                        wait(pe, dve_xlo, u + 1)
                    for c in range(DC):
                        last = nc.tensor.matmul(p_qk[:], x[:, c * P:(c + 1) * P],
                                                w[:, c * 3 * D:c * 3 * D + 2 * D],
                                                start=n == 0 and c == 0, stop=n == 2 and c == DC - 1)
                last.then_inc(pe_qk, 1)
                wait(pe, act_av, u - 2)
                for n, (w, x) in enumerate(three_passes(w_qkv_parts, xnT_parts)):
                    for c in range(DC):
                        last = nc.tensor.matmul(p_v[:, 0:D], x[:, c * P:(c + 1) * P],
                                                w[:, c * 3 * D + 2 * D:(c + 1) * 3 * D],
                                                start=n == 0 and c == 0, stop=n == 2 and c == DC - 1)
                last.then_inc(pe_v, 1)

            def transpose_probs(u, j):
                wait(pe, act_pT, 2 * u)
                wait(pe, act_qkT, min_pair(u + 2))
                for half, dst in enumerate((p_pT, p_mix)):
                    wait(pe, pool_norm, 2 * u + half + 1)
                    for g in range(4):
                        head = 2 * (4 * half + g)
                        last = nc.tensor.transpose(dst[:, g * P:(g + 1) * P],
                                                   probs[j][:, head * TP:(head + 2) * TP], ident)
                    last.then_inc(pe_pT, 1)

            def attend(u):
                wait(pe, act_vb, 4 * (u + 1))
                wait(pe, act_v, min_pair(u + 3))
                for half in range(2):
                    wait(pe, act_pT, 2 * u + half + 1)
                    for b in range(IMGS):
                        for g in range(4):
                            col = D + half * P + b * TP
                            vb = (b * HC + 4 * half + g) * 2 * HD
                            last = nc.tensor.matmul(
                                p_v[32 * g:32 * (g + 1), col:col + TP], v_blocks[:, vb:vb + 2 * HD],
                                probsT[:, (4 * half + g) * P + b * TP:(4 * half + g) * P + (b + 1) * TP],
                                start=True, stop=True)
                last.then_inc(pe_av, 1)

            def second_rows(u, j):
                wait(pe, dve_xn2, u + 1)
                wait(pe, dve_xlo, min_pair(u + 4))
                transpose_rows(xn2[j], pe_x2T)

            def project(u):
                wait(pe, act_av, u + 1)
                wait(pe, dve_h, min_pair(u + 5))
                for c in range(DC):
                    last = nc.tensor.matmul(p_h[:, D:2 * D], attnT[:, c * P:(c + 1) * P],
                                            w_proj[:, c * D:(c + 1) * D], start=c == 0, stop=c == DC - 1)
                last.then_inc(pe_proj, 1)

            def route(u):
                wait(pe, act_x2T, u + 1)
                wait(pe, act_lg, u)
                wait(pe, dve_mask, 2 * min_pair(u + 3) - 1)
                for c in range(DC):
                    last = nc.tensor.matmul(p_s[:, SC:SC + E], xn2T[:, c * P:(c + 1) * P],
                                            w_router[:, c * E:(c + 1) * E], start=c == 0, stop=c == DC - 1)
                last.then_inc(pe_lg, 1)

            def transpose_qk(u):
                wait(pe, dve_rot, u + 1)
                wait(pe, act_pT, 2 * (u - 1))
                for c in range(4):
                    last = nc.tensor.transpose(p_mix[:, c * P:(c + 1) * P], qk_rot[:, c * P:(c + 1) * P], ident)
                last.then_inc(pe_qkT, 1)

            def score(u):
                wait(pe, act_qkT, u + 1)
                wait(pe, act_lg, u - 2)
                for c in range(DC):
                    wait(pe, dve_mask, 2 * u - 1 + c)
                    wait(pe, pool_kb, 2 * u + c + 1)
                    for b in range(IMGS):
                        last = nc.tensor.matmul(p_s[b * TP:(b + 1) * TP, c * 512:c * 512 + SC],
                                                qkT[:, c * P + b * TP:c * P + (b + 1) * TP],
                                                k_blocks[:, (c * IMGS + b) * SC:(c * IMGS + b + 1) * SC],
                                                start=True, stop=True)
                    last.then_inc(pe_s, 1)

            def step(t, j):
                if exists(t, PAIRS):
                    first_rows(t, j)
                    if exists(t - 4, PAIRS):
                        route(t - 4)
                if exists(t - 3, PAIRS):
                    project(t - 3)
                if isinstance(t, int) and t >= PAIRS:
                    route(t - 4)
                if exists(t, PAIRS):
                    if isinstance(t, int) and t == 0:
                        pe.wait_ge(act_whi, W_CUTS + 1)
                        pe.wait_ge(dve_wlo, W_CUTS + 1)
                        pe.wait_ge(s_wqkv, 16 * 3)
                    qkv(t)
                last_scores = isinstance(t, int) and t == PAIRS
                if last_scores:
                    score(t - 1)
                if exists(t - 2, PAIRS):
                    transpose_probs(t - 2, j)
                if exists(t - 1, PAIRS) and not last_scores:
                    score(t - 1)
                if exists(t, PAIRS):
                    transpose_qk(t)
                if exists(t - 2, PAIRS) and not exists(t + 2, PAIRS):
                    attend(t - 2)
                if exists(t - 3, PAIRS):
                    second_rows(t - 3, 1 - j)
                if exists(t + 2, PAIRS):
                    embed(t + 2, j)
                if exists(t - 2, PAIRS) and exists(t + 2, PAIRS):
                    attend(t - 2)

            run_steps(pe, step, -2, 6, 30, PAIRS + 4)

        @block.scalar
        def _(act):
            def patches_high(u, j):
                wait(act, s_pat[j], pair_loads(u, j))
                wait(act, pe_h, u - 1)
                nc.scalar.copy(view(patch_parts[j][0], 0, P, 0, [[P, KC], [TP, IMGS], [1, T]]),
                               view(patches[j], 0, P, 0, [[PATCH_COLS, KC], [T, IMGS], [1, T]])
                               ).then_inc(act_phi, 1)

            def second_rows_out(u):
                wait(act, pe_x2T, u + 1)
                nc.scalar.copy(xn2T[:], p_xT[:, 0:D]).then_inc(act_x2T, 1)

            def attention_out(u):
                wait(act, pe_av, u + 1)
                nc.scalar.copy(attnT[:], p_v[:, D:2 * D]).then_inc(act_av, 1)

            def exponentials(u, j, c):
                wait(act, dve_shift, 2 * u + c + 1)
                wait(act, pe_pT, 2 * (u - 2) + c + 1)
                nc.scalar.activation(view(probs[j], 0, P, c * HC * TP, [[TP, HC], [1, T]]),
                                     view(scores, 0, P, c * SC, [[T, HC], [1, T]]),
                                     ACT.Exp, scale=float(HD) ** -0.5).then_inc(act_exp, 1)

            def step(t, j):
                if exists(t, PAIRS):
                    wait(act, pe_xT, t + 1)
                    wait(act, pe_v, t)
                    wait(act, dve_xlo, t)
                    nc.scalar.copy(xnT_parts[0][:], p_xT[:, 0:D]).then_inc(act_xT, 1)
                if exists(t - 4, PAIRS):
                    wait(act, pe_lg, t - 3)
                    nc.scalar.copy(logits[:, bass.ds((t - 4) * E, E)], p_s[:, SC:SC + E]).then_inc(act_lg, 1)
                if exists(t - 2, PAIRS):
                    wait(act, act_v, t - 1)
                    wait(act, pe_av, t - 2)
                    for half in range(2):
                        for b in range(IMGS):
                            nc.scalar.copy(
                                view(v_blocks, TP * half, TP, b * HC * 2 * HD + half * HD, [[2 * HD, HC], [1, HD]]),
                                view(v_rows[j], TP * b, TP, half * HD, [[2 * HD, HC], [1, HD]]),
                            ).then_inc(act_vb, 1)
                if exists(t + 3, PAIRS) and not (isinstance(t, int) and t < -1):
                    patches_high(t + 3, 1 - j)
                if exists(t, PAIRS):
                    wait(act, pe_v, t + 1)
                    wait(act, act_vb, 4 * (t - 1))
                    nc.scalar.copy(v_rows[j][:], p_v[:, 0:D]).then_inc(act_v, 1)
                if exists(t - 2, PAIRS):
                    for half, src in enumerate((p_pT, p_mix)):
                        wait(act, pe_pT, 2 * (t - 2) + half + 1)
                        nc.scalar.copy(probsT[:, half * 512:(half + 1) * 512], src[:]).then_inc(act_pT, 1)
                if exists(t, PAIRS):
                    wait(act, pe_qkT, t + 1)
                    wait(act, pool_kb, 2 * t)
                    nc.scalar.copy(qkT[:], p_mix[:]).then_inc(act_qkT, 1)
                if exists(t - 3, PAIRS) and exists(t + 2, PAIRS):
                    second_rows_out(t - 3)
                if exists(t - 2, PAIRS) and not exists(t + 2, PAIRS):
                    attention_out(t - 2)
                if exists(t - 3, PAIRS) and not exists(t + 2, PAIRS):
                    second_rows_out(t - 3)
                if exists(t - 1, PAIRS):
                    exponentials(t - 1, 1 - j, 0)
                    exponentials(t - 1, 1 - j, 1)
                if exists(t - 2, PAIRS) and exists(t + 2, PAIRS):
                    attention_out(t - 2)

            act.wait_ge(s_zero, 2)
            patches_high(0, 0)
            for k in range(W_CUTS):
                act.wait_ge(s_wtok[k], 16)
                nc.scalar.copy(a_cut(w_tok_parts[0], k), a_cut(w_tok, k)).then_inc(act_whi, 1)
            act.wait_ge(s_wq, 16)
            nc.scalar.copy(w_qkv_parts[0][:], w_qkv[:]).then_inc(act_whi, 1)
            act.wait_ge(s_zero, 4)
            patches_high(1, 1)
            act.wait_ge(s_clear, 3)
            run_steps(act, step, -2, 6, 26, PAIRS + 4)

        @block.vector
        def _(dve):
            def add_mask(u, c):
                wait(dve, pe_s, 2 * u + c + 1)
                wait(dve, act_exp, 2 * u - 1 + c)
                nc.vector.tensor_tensor(view(scores, 0, P, c * SC, [[T, HC], [1, T]]),
                                        view(p_s, 0, P, c * 512, [[T, HC], [1, T]]),
                                        view(consts, 0, P, C_CAUSAL, [[0, HC], [1, T]]),
                                        ALU.add).then_inc(dve_mask, 1)

            def softmax_max(u):
                wait(dve, dve_mask, 2 * (u + 1))
                nc.vector.tensor_reduce(row_max[:], view(scores, 0, P, 0, [[T, HEADS], [1, T]]), AX,
                                        ALU.max).then_inc(dve_max, 1)

            def subtract_max(u, c):
                wait(dve, dve_max, u + 1)
                s3 = view(scores, 0, P, c * SC, [[T, HC], [1, T]])
                nc.vector.tensor_tensor(s3, s3, view(row_max, 0, P, c * HC, [[1, HC], [0, T]]),
                                        ALU.subtract).then_inc(dve_shift, 1)

            def rope_cos(u):
                wait(dve, pe_qk, u + 1)
                nc.vector.tensor_tensor(view(qk_cos, 0, P, 0, [[HD, 2 * HEADS], [1, HD]]),
                                        view(p_qk, 0, P, 0, [[HD, 2 * HEADS], [1, HD]]),
                                        view(consts, 0, P, C_COS, [[0, 2 * HEADS], [1, HD]]),
                                        ALU.mult).then_inc(dve_rope, 1)

            def rope_sin(u):
                half = HD // 2
                nc.vector.tensor_tensor(view(qk_sin, 0, P, 0, [[HD, 2 * HEADS], [half, 2], [1, half]]),
                                        view(p_qk, 0, P, half, [[HD, 2 * HEADS], [-half, 2], [1, half]]),
                                        view(consts, 0, P, C_SIN, [[0, 2 * HEADS], [half, 2], [1, half]]),
                                        ALU.mult).then_inc(dve_rope, 1)

            def add_eps(u, mom, ve, s_mom, s_eps, s_used):
                wait(dve, s_mom, u + 1)
                wait(dve, s_used, u)
                nc.vector.tensor_scalar(ve[:], mom[:, 1:2], EPS, None, ALU.add).then_inc(s_eps, 1)

            def rope_add(u):
                wait(dve, dve_rope, 2 * (u + 1))
                wait(dve, pe_qkT, u)
                nc.vector.tensor_tensor(qk_rot[:], qk_cos[:], qk_sin[:], ALU.add).then_inc(dve_rot, 1)

            def fence(col):
                nc.vector.memset(fences[:, col:col + 1], 0.0)

            def normalise(u, dst, mom, rs, done):
                nc.vector.tensor_scalar(dst[:], h_all[:, bass.ds(u * D, D)], mom[:, 0:1], rs[:, 0:1],
                                        ALU.subtract, ALU.mult).then_inc(done, 1)

            def step(t, j):
                if exists(t - 3, PAIRS):
                    h_rest = h_all[:, bass.ds((t - 3) * D, D)]
                    wait(dve, pe_proj, t - 2)
                    wait(dve, pool_bias, t - 2)
                    nc.vector.tensor_tensor(h_rest, p_h[:, D:2 * D], h_rest, ALU.add).then_inc(dve_res, 1)
                    wait(dve, dve_res, t - 2)
                    fence(0)
                    nc.vector.bn_stats(stats2[:], h_rest).then_inc(dve_st2, 1)
                if exists(t, PAIRS):
                    rope_cos(t)
                if exists(t - 3, PAIRS):
                    wait(dve, dve_st2, t - 2)
                    fence(1)
                    nc.vector.bn_aggr(moments2[:], stats2[:]).then_inc(dve_mom2, 1)
                if exists(t, PAIRS):
                    rope_sin(t)
                if exists(t - 3, PAIRS):
                    add_eps(t - 3, moments2, var_eps2, dve_mom2, dve_eps2, pool_rstd2)
                if exists(t, PAIRS):
                    rope_add(t)
                if exists(t - 1, PAIRS):
                    add_mask(t - 1, 0)
                if exists(t - 3, PAIRS):
                    wait(dve, pool_rstd2, t - 2)
                    wait(dve, pe_x2T, t - 4)
                    wait(dve, s_store[1 - j], stored(t - 5, j))
                    normalise(t - 3, xn2[1 - j], moments2, rstd2, dve_xn2)
                if exists(t - 1, PAIRS):
                    add_mask(t - 1, 1)
                    softmax_max(t - 1)
                    subtract_max(t - 1, 0)
                if exists(t + 1, PAIRS):
                    wait(dve, pool_rstd, t + 2)
                    wait(dve, pe_xT, t)
                    normalise(t + 1, xn[1 - j], moments, rstd, dve_xn)
                if exists(t - 1, PAIRS):
                    subtract_max(t - 1, 1)
                if exists(t + 2, PAIRS):
                    h_rows = h_all[:, bass.ds((t + 2) * D, D)]
                    wait(dve, pe_h, t + 3)
                    nc.vector.tensor_tensor(h_rows, p_h[:, 0:D], b_tok[:], ALU.add).then_inc(dve_h, 1)
                if exists(t - 1, PAIRS):
                    for c in range(DC):
                        wait(dve, act_exp, 2 * (t - 1) + c + 1)
                        nc.vector.tensor_reduce(row_sum[:, c * HC:(c + 1) * HC],
                                                view(probs[1 - j], 0, P, c * HC * TP, [[TP, HC], [1, T]]), AX,
                                                ALU.add).then_inc(dve_sum, 1)
                if exists(t + 2, PAIRS):
                    wait(dve, dve_h, t + 3)
                    fence(2)
                    nc.vector.bn_stats(stats[:], h_rows).then_inc(dve_st, 1)
                if exists(t - 1, PAIRS):
                    wait(dve, dve_sum, 2 * t)
                    wait(dve, pool_norm, 2 * (t - 1))
                    nc.vector.reciprocal(row_inv[:], row_sum[:]).then_inc(dve_inv, 1)
                if exists(t + 2, PAIRS):
                    wait(dve, dve_st, t + 3)
                    fence(3)
                    nc.vector.bn_aggr(moments[:], stats[:]).then_inc(dve_mom, 1)
                if exists(t + 1, PAIRS):
                    wait(dve, act_xT, t + 2)
                    wait(dve, pe_v, t + 1)
                    nc.vector.tensor_tensor(xnT_parts[1][:], p_xT[:, 0:D], xnT_parts[0][:].bitcast(F32),
                                            ALU.subtract).then_inc(dve_xlo, 1)
                if exists(t + 2, PAIRS):
                    add_eps(t + 2, moments, var_eps, dve_mom, dve_eps, pool_rstd)

            def stored(u, j):
                if isinstance(u, int):
                    return (u // 2 + 1) * 16 if u >= 0 else 0
                return (u - (1 - j)) * 8 + 16

            for k in range(W_CUTS):
                dve.wait_ge(act_whi, k + 1)
                nc.vector.tensor_tensor(a_cut(w_tok_parts[1], k), a_cut(w_tok, k),
                                        a_cut(w_tok_parts[0], k).bitcast(F32), ALU.subtract).then_inc(dve_wlo, 1)
            dve.wait_ge(act_whi, W_CUTS + 1)
            nc.vector.tensor_tensor(w_qkv_parts[1][:], w_qkv[:], w_qkv_parts[0][:].bitcast(F32),
                                    ALU.subtract).then_inc(dve_wlo, 1)
            dve.wait_ge(s_w, 16 * 2)
            run_steps(dve, step, *LOOP)

        @block.gpsimd
        def _(pool):
            for tile in patch_parts[0] + patch_parts[1]:
                nc.gpsimd.memset(tile[:].bitcast(F32), 0.0).then_inc(s_zero, 1)
            nc.gpsimd.memset(minus_half[:], -0.5).then_inc(s_zero, 1)
            pool.wait_ge(s_zero, N_ZERO)
            def patches_low(u, j):
                wait(pool, act_phi, u + 1)
                wait(pool, pe_h, u - 1)
                cols = [[P, KC], [TP, IMGS], [1, T]]
                nc.gpsimd.tensor_tensor(view(patch_parts[j][1], 0, P, 0, cols),
                                        view(patches[j], 0, P, 0, [[PATCH_COLS, KC], [T, IMGS], [1, T]]),
                                        view(patch_parts[j][0], 0, P, 0, cols, F32), ALU.subtract).then_inc(pool_plo, 1)

            def inverse_std(u, ve, rs, s_eps, s_rstd, s_used):
                wait(pool, s_eps, u + 1)
                wait(pool, s_used, u)
                nc.gpsimd.tensor_tensor(rs[:], ve[:], minus_half[:], ALU.pow).then_inc(s_rstd, 1)

            def step(t, j):
                if exists(t, PAIRS):
                    wait(pool, dve_xn, t + 1)
                    h_rows = h_all[:, bass.ds(t * D, D)]
                    nc.gpsimd.tensor_tensor(h_rows, h_rows, b_proj[:], ALU.add).then_inc(pool_bias, 1)
                if exists(t - 3, PAIRS):
                    inverse_std(t - 3, var_eps2, rstd2, dve_eps2, pool_rstd2, dve_xn2)
                if exists(t + 1, PAIRS):
                    inverse_std(t + 1, var_eps, rstd, dve_eps, pool_rstd, dve_xn)
                if exists(t, PAIRS):
                    wait(pool, act_qkT, t + 1)
                    wait(pool, pe_s, 2 * t)
                    for c in range(DC):
                        nc.gpsimd.tensor_tensor(
                            view(k_blocks, 0, P, c * IMGS * SC, [[SC, IMGS], [T, HC], [1, T]]),
                            view(qkT, 0, P, (DC + c) * P, [[TP, IMGS], [0, HC], [1, T]]),
                            view(consts, 0, P, C_HEAD, [[0, IMGS], [1, HC], [0, T]]),
                            ALU.mult).then_inc(pool_kb, 1)
                if exists(t + 3, PAIRS) and not (isinstance(t, int) and t < -1):
                    patches_low(t + 3, 1 - j)
                if exists(t - 1, PAIRS):
                    wait(pool, dve_inv, t)
                    for c in range(DC):
                        pr = view(probs[1 - j], 0, P, c * HC * TP, [[TP, HC], [1, T]])
                        nc.gpsimd.tensor_tensor(pr, pr, view(row_inv, 0, P, c * HC, [[1, HC], [0, T]]),
                                                ALU.mult).then_inc(pool_norm, 1)

            for tile in (v_blocks, probs[0], probs[1]):
                nc.gpsimd.memset(tile[:], 0.0).then_inc(s_clear, 1)
            patches_low(0, 0)
            patches_low(1, 1)
            pool.wait_ge(s_w, 16 * 2)
            pool.wait_ge(s_wqkv, 16 * 3)
            run_steps(pool, step, -2, 6, 26, PAIRS + 3)


def build_routing(nc, io, logits, consts, expert_weights, chosen_gate, slot_parts, slot_angles):
    with ExitStack() as ctx:
        def sb(name, cols, rows=P):
            return ctx.enter_context(nc.sbuf_tensor(name, [rows, cols], F32))

        def sem(name):
            return ctx.enter_context(nc.semaphore(name))

        HALVES = 2
        HALF = PAIRS // HALVES
        SETS = HALVES * IMGS
        RING = 4
        PARTS = 4
        QC = QUAD * E * PS
        gates = sb("gates", PAIRS * E)
        chosen = sb("chosen", PAIRS * E * PS)
        gate_rows = sb("gate_rows", SETS * TP)
        code_rows = sb("code_rows", SETS * TP)
        code_cols = sb("code_cols", PAIRS * E)
        top8 = sb("top8", SETS * 8)
        above = sb("above", SETS * T)
        ties = sb("ties", SETS * T)
        tie_rank = sb("tie_rank", SETS * T)
        taken = sb("taken", SETS * T)
        order = sb("order", SETS * T)
        room = sb("room", SETS)
        zeros = sb("zeros", T)
        rows = [sb(f"rows{j}", QUAD * D) for j in range(RING)]
        p_rows = ctx.enter_context(nc.psum_tensor("p_rows", [P, 512], F32))
        p_cols = ctx.enter_context(nc.psum_tensor("p_cols", [P, 512], F32))
        banks = [[ctx.enter_context(nc.psum_tensor(f"p_g{j}{c}", [P, 512], F32)) for c in range(DC + 1)]
                 for j in range(2)]
        r_exp, r_one, r_gate, r_rowsT, r_rows, r_zero, r_codeT, r_code, r_cols, r_clear, r_chosen, r_sel = (
            sem(n) for n in ("r_exp", "r_one", "r_gate", "r_rowsT", "r_rows", "r_zero", "r_codeT", "r_code",
                             "r_cols", "r_clear", "r_chosen", "r_sel"))
        g_in = [sem(f"g_in{j}") for j in range(RING)]
        g_mm, g_act, g_dve = sem("g_mm"), sem("g_act"), sem("g_dve")
        block = ctx.enter_context(nc.Block())

        @block.sync
        def _(sp):
            def load(q, j):
                wait(sp, g_mm, q - RING + 1)
                sp.dma_start(rows[j][:].rearrange("p (q n) -> p q n", q=QUAD),
                             io["xn2_dram"][bass.ds(q * QUAD, QUAD)].rearrange("q p n -> p q n")
                             ).then_inc(g_in[j], 16)

            for q in range(RING):
                load(q, q)
            for e in range(2):
                load_expert_qkv(sp, io, expert_weights, e)
                load_expert_out(sp, io, expert_weights, e)
            for q in range(RING, NQ):
                load(q, q % RING)

        @block.tensor
        def _(pe):
            ident = consts[:, C_ID:C_ID + P]
            pe.wait_ge(r_gate, 1)
            for h in range(HALVES):
                last = nc.tensor.transpose(p_rows[:, h * P:(h + 1) * P],
                                           gates[:, h * HALF * E:(h + 1) * HALF * E], ident)
            last.then_inc(r_rowsT, 1)
            keep_clock_up(nc, consts, banks[0][0], 20)
            pe.wait_ge(r_code, 1)
            for h in range(HALVES):
                last = nc.tensor.transpose(p_cols[:, h * P:(h + 1) * P], code_rows[:, h * P:(h + 1) * P], ident)
            last.then_inc(r_codeT, 1)
            keep_clock_up(nc, consts, banks[0][0], 6)

            def gather(q, k, first):
                pe.wait_ge(g_in[k], 16 if first else 32)
                pe.wait_ge(r_chosen, IMGS * (k // 2 + (1 if first else 1 + PARTS // 2)))
                wait(pe, g_dve, (q - 1) * (DC + 1))
                for n in range(QUAD):
                    for c in range(DC):
                        nc.tensor.matmul(banks[k % 2][c][:, n * E * PS:(n + 1) * E * PS],
                                         rows[k][:, n * D + c * P:n * D + (c + 1) * P],
                                         chosen[:, bass.ds(q * QC + n * E * PS, E * PS)], start=True, stop=True)
                nc.tensor.matmul(banks[k % 2][DC][:, 0:QC], consts[:, C_ROT:C_ROT + P],
                                 chosen[:, bass.ds(q * QC, QC)], start=True, stop=True).then_inc(g_mm, 1)

            for q in range(RING):
                gather(q, q, True)
            for q in range(RING, NQ):
                gather(q, q % RING, False)

            keep_clock_up(nc, consts, p_rows, 8)

        def by_expert(dst, base, q, dtype=None):
            return view(dst, 0, P, q * (QUAD * PS) + base, [[PS, QUAD], [NS, E], [1, PS]], dtype)

        def by_pair(src):
            return view(src, 0, P, 0, [[E * PS, QUAD], [PS, E], [1, PS]])

        @block.scalar
        def _(act):
            nc.scalar.activation(gates[:], logits[:], ACT.Exp, scale=-1.0).then_inc(r_exp, 1)
            expert_weights_high(nc, act, expert_weights, 0)
            with act.Fori(0, NQ // 2) as i:
                for j in range(2):
                    q = i * 2 + j
                    act.wait_ge(g_mm, q + 1)
                    for c in range(DC):
                        nc.scalar.copy(by_expert(slot_parts[0], c * E * NS, q),
                                       by_pair(banks[j][c])).then_inc(g_act, 1)

        @block.vector
        def _(dve):
            dve.wait_ge(r_exp, 1)
            nc.vector.tensor_scalar(gates[:], gates[:], 1.0, None, ALU.add).then_inc(r_one, 1)
            dve.wait_ge(r_one, 1)
            nc.vector.reciprocal(gates[:], gates[:]).then_inc(r_gate, 1)
            dve.wait_ge(r_rowsT, 1)
            nc.vector.tensor_copy(gate_rows[:], p_rows[:, 0:SETS * TP]).then_inc(r_rows, 1)
            dve.wait_ge(r_rows, 1)
            dve.wait_ge(r_zero, 2)
            done = 0

            def settle(*ops):
                nonlocal done
                for op in ops:
                    op.then_inc(r_sel, 1)
                done += len(ops)
                dve.wait_ge(r_sel, done)

            def every(tile, pitch=T):
                return view(tile, 0, P, 0, [[pitch, SETS], [1, T]])

            def a_set(tile, k, pitch=T):
                return tile[:, k * pitch:k * pitch + T]

            def per_set(tile, off, pitch):
                return view(tile, 0, P, off, [[pitch, SETS], [0, T]])

            cut = per_set(top8, SLOTS - 1, 8)
            settle(*[nc.vector.max(top8[:, k * 8:(k + 1) * 8], a_set(gate_rows, k, TP)) for k in range(SETS)])
            settle(nc.vector.tensor_tensor(every(above), every(gate_rows, TP), cut, ALU.is_gt),
                   nc.vector.tensor_tensor(every(ties), every(gate_rows, TP), cut, ALU.is_equal))
            settle(nc.vector.tensor_reduce(room[:], every(above), AX, ALU.add),
                   *[nc.vector.tensor_tensor_scan(a_set(tie_rank, k), a_set(ties, k), zeros[:], 0.0,
                                                  ALU.add, ALU.add) for k in range(SETS)])
            settle(nc.vector.tensor_scalar(room[:], room[:], -1.0, float(SLOTS), ALU.mult, ALU.add))
            settle(nc.vector.tensor_tensor(every(taken), every(tie_rank), per_set(room, 0, 1), ALU.is_le))
            settle(nc.vector.tensor_tensor(every(taken), every(taken), every(ties), ALU.mult))
            settle(nc.vector.tensor_tensor(every(taken), every(taken), every(above), ALU.add))
            settle(*[nc.vector.tensor_tensor_scan(a_set(order, k), a_set(taken, k), zeros[:], 0.0,
                                                  ALU.add, ALU.add) for k in range(SETS)])
            nc.vector.tensor_tensor(every(code_rows, TP), every(order), every(taken), ALU.mult).then_inc(r_code, 1)
            dve.wait_ge(r_codeT, 1)
            nc.vector.tensor_copy(code_cols[:], p_cols[:, 0:PAIRS * E]).then_inc(r_cols, 1)
            dve.wait_ge(r_cols, 1)
            dve.wait_ge(r_clear, 1)
            n = PAIRS * E // PARTS
            for part in range(PARTS):
                for b in range(IMGS):
                    nc.vector.tensor_tensor(
                        view(chosen, b * TP, TP, part * n * PS + b * SLOTS, [[PS, n], [1, SLOTS]]),
                        view(code_cols, b * TP, TP, part * n, [[1, n], [0, SLOTS]]),
                        view(consts, b * TP, TP, C_SLOT, [[0, n], [1, SLOTS]]),
                        ALU.is_equal).then_inc(r_chosen, 1)
            with dve.Fori(0, NQ // 2) as i:
                for j in range(2):
                    q = i * 2 + j
                    dve.wait_ge(g_mm, q + 1)
                    nc.vector.tensor_copy(by_expert(slot_angles, 0, q), by_pair(banks[j][DC])).then_inc(g_dve, 1)
                    for c in range(DC):
                        dve.wait_ge(g_act, q * DC + c + 1)
                        nc.vector.tensor_tensor(by_expert(slot_parts[1], c * E * NS, q), by_pair(banks[j][c]),
                                                by_expert(slot_parts[0], c * E * NS, q, F32),
                                                ALU.subtract).then_inc(g_dve, 1)

        @block.gpsimd
        def _(pool):
            nc.gpsimd.memset(code_rows[:], 0.0).then_inc(r_zero, 1)
            nc.gpsimd.memset(zeros[:], 0.0).then_inc(r_zero, 1)
            nc.gpsimd.memset(chosen[:], 0.0).then_inc(r_clear, 1)
            pool.wait_ge(r_chosen, IMGS * PARTS)
            nc.gpsimd.tensor_tensor(view(chosen_gate, 0, P, 0, [[PS, PAIRS * E], [1, PS]]),
                                    view(chosen, 0, P, 0, [[PS, PAIRS * E], [1, PS]]),
                                    view(gates, 0, P, 0, [[1, PAIRS * E], [0, PS]]), ALU.mult)
            expert_weights_low(nc, pool, expert_weights, 0)


class ExpertWeights:

    def __init__(self, nc, ctx):
        def sb(name, cols, dtype=F32):
            return ctx.enter_context(nc.sbuf_tensor(name, [P, cols], dtype))

        self.high = [sb(f"w_e_hi{j}", DC * 3 * HP, F32R) for j in range(2)]
        self.low = [sb(f"w_e_lo{j}", DC * 3 * HP, F32R) for j in range(2)]
        self.high_made = ctx.enter_context(nc.semaphore("e_high"))
        self.low_made = ctx.enter_context(nc.semaphore("e_low"))
        self.qkv = [sb(f"w_e{j}", DC * 3 * HP) for j in range(2)]
        self.out = [sb(f"wo_e{j}", D) for j in range(4)]
        self.qkv_in = [ctx.enter_context(nc.semaphore(f"e_qkv{j}")) for j in range(2)]
        self.out_in = [ctx.enter_context(nc.semaphore(f"e_out{j}")) for j in range(4)]


def expert_weights_high(nc, act, weights, e):
    act.wait_ge(weights.qkv_in[e % 2], 16 * (e // 2 + 1))
    nc.scalar.copy(weights.high[e % 2][:], weights.qkv[e % 2][:]).then_inc(weights.high_made, 1)


def expert_weights_low(nc, pool, weights, e):
    pool.wait_ge(weights.high_made, e + 1)
    nc.gpsimd.tensor_tensor(weights.low[e % 2][:], weights.qkv[e % 2][:], weights.high[e % 2][:].bitcast(F32),
                            ALU.subtract).then_inc(weights.low_made, 1)


def load_expert_qkv(sp, io, weights, e):
    sp.dma_start(weights.qkv[e % 2][:].rearrange("p (c n) -> p c n", c=DC),
                 io["L0_ffn_Wqkv"][e].rearrange("(c p) n -> p c n", p=P)).then_inc(weights.qkv_in[e % 2], 16)


def load_expert_out(sp, io, weights, e):
    sp.dma_start(weights.out[e % 4][:], io["L0_ffn_Wo"][e]).then_inc(weights.out_in[e % 4], 16)


def build_experts(nc, io, consts, weights, slot_parts, slot_angles, slot_out):
    with ExitStack() as ctx:
        def sb(name, cols, rows=P):
            return ctx.enter_context(nc.sbuf_tensor(name, [rows, cols], F32))

        def sem(name):
            return ctx.enter_context(nc.semaphore(name))

        wo_e = weights.out
        turned = sb("turned", 2 * NS)
        straight = sb("straight", 2 * NS, 2 * ROT)
        qk = [sb(f"qk{j}", 2 * NS) for j in range(2)]
        v = [sb(f"v{j}", NG * HP, GS) for j in range(4)]
        s_e = sb("s_e", NG * GS, GS)
        a_e = sb("a_e", NG * GS, GS)
        aT = sb("aT", NG * GS, GS)
        avT = sb("avT", NS)
        mx = sb("mx", NG, GS)
        sm = sb("sm", NG, GS)
        inv = sb("inv", NG, GS)
        p_qk = ctx.enter_context(nc.psum_tensor("p_qke", [P, 1024], F32))
        p_v, p_s, p_aT, p_av = (ctx.enter_context(nc.psum_tensor(n, [P, 512], F32))
                                for n in ("p_ve", "p_se", "p_aTe", "p_ave"))
        p_o = ctx.enter_context(nc.psum_tensor("p_oe", [P, 1024], F32))
        (m_qk, m_v, m_s, m_aT, m_av, m_o) = (sem(n) for n in ("m_qk", "m_v", "m_s", "m_aT", "m_av", "m_o"))
        (a_rest, a_v, a_exp, a_aT, a_av, a_o) = (sem(n) for n in ("a_rest", "a_v", "a_exp", "a_aT", "a_av", "a_o"))
        (d_turn, d_rope, d_mask, d_max, d_shift, d_sum, d_inv, d_norm) = (
            sem(n) for n in ("d_turn", "d_rope", "d_mask", "d_max", "d_shift", "d_sum", "d_inv", "d_norm"))
        g_s = sem("g_s")
        block = ctx.enter_context(nc.Block())

        def run(eng, step):
            for t in range(E + 2):
                step(t, t % 2)

        @block.sync
        def _(sp):
            for e in range(2, E):
                wait(sp, weights.low_made, e - 1)
                load_expert_qkv(sp, io, weights, e)
                wait(sp, m_o, e - 3)
                load_expert_out(sp, io, weights, e)

        @block.tensor
        def _(pe):
            ident = consts[:, C_ID:C_ID + P]

            def transpose_attention(u):
                wait(pe, d_norm, u + 1)
                wait(pe, a_aT, u)
                for g in range(NG):
                    last = nc.tensor.transpose(p_aT[0:GS, g * GS:(g + 1) * GS],
                                               a_e[:, g * GS:(g + 1) * GS], ident[0:GS, 0:GS])
                last.then_inc(m_aT, 1)

            def queries_keys(u, j):
                wait(pe, weights.high_made, u + 1)
                wait(pe, weights.low_made, u + 1)
                wait(pe, a_rest, u)
                wait(pe, d_turn, 2 * u)
                wait(pe, d_rope, 2 * u)
                for k in range(2):
                    for n, (w, x) in enumerate(three_passes((weights.high[j], weights.low[j]), slot_parts)):
                        for c in range(DC):
                            last = nc.tensor.matmul(p_qk[:, k * 512:k * 512 + NS],
                                                    w[:, c * 3 * HP + k * HP:c * 3 * HP + (k + 1) * HP],
                                                    x[:, (c * E + u) * NS:(c * E + u + 1) * NS],
                                                    start=n == 0 and c == 0, stop=n == 2 and c == DC - 1)
                last.then_inc(m_qk, 1)

            def values(u, j):
                wait(pe, a_v, u)
                for g in range(NG):
                    for n, (w, x) in enumerate(three_passes((weights.high[j], weights.low[j]), slot_parts)):
                        for c in range(DC):
                            x0 = (c * E + u) * NS + g * GS
                            last = nc.tensor.matmul(p_v[0:GS, g * HP:(g + 1) * HP], x[:, x0:x0 + GS],
                                                    w[:, c * 3 * HP + 2 * HP:(c + 1) * 3 * HP],
                                                    start=n == 0 and c == 0, stop=n == 2 and c == DC - 1)
                last.then_inc(m_v, 1)

            def scores(u, j):
                wait(pe, g_s, u + 1)
                wait(pe, a_rest, u + 1)
                wait(pe, d_mask, u)
                for g in range(NG):
                    last = nc.tensor.matmul(p_s[0:GS, g * GS:(g + 1) * GS], qk[j][:, g * GS:(g + 1) * GS],
                                            qk[j][:, NS + g * GS:NS + (g + 1) * GS], start=True, stop=True)
                last.then_inc(m_s, 1)

            def attend(u):
                wait(pe, a_aT, u + 1)
                wait(pe, a_v, u + 1)
                wait(pe, a_av, u)
                for g in range(NG):
                    last = nc.tensor.matmul(p_av[:, g * GS:(g + 1) * GS], v[u % 4][:, g * HP:(g + 1) * HP],
                                            aT[:, g * GS:(g + 1) * GS], start=True, stop=True)
                last.then_inc(m_av, 1)

            def project(u):
                wait(pe, a_av, u + 1)
                wait(pe, weights.out_in[u % 4], 16 * (u // 4 + 1))
                wait(pe, a_o, DC * u)
                for c in range(DC):
                    last = nc.tensor.matmul(p_o[:, c * 512:c * 512 + NS], wo_e[u % 4][:, c * P:(c + 1) * P],
                                            avT[:], start=True, stop=True)
                last.then_inc(m_o, 1)

            def step(t, j):
                if exists(t, E):
                    queries_keys(t, j)
                if exists(t - 2, E):
                    transpose_attention(t - 2)
                if exists(t - 1, E):
                    scores(t - 1, 1 - j)
                if exists(t - 2, E):
                    attend(t - 2)
                if exists(t, E):
                    values(t, j)
                if exists(t - 2, E):
                    project(t - 2)
                if t == E:
                    keep_clock_up(nc, consts, p_qk, 8)

            run(pe, step)

        def leave(copy, u, c):
            return copy(view(slot_out, 0, P, (c * E + u) * PS, [[DC * E * PS, PAIRS], [1, PS]]),
                        view(p_o, 0, P, c * 512, [[PS, PAIRS], [1, PS]]))

        @block.scalar
        def _(act):
            def step(t, j):
                if exists(t + 1, E):
                    wait(act, m_v, t)
                    expert_weights_high(nc, act, weights, t + 1)
                if exists(t - 2, E):
                    wait(act, m_aT, t - 1)
                    nc.scalar.copy(aT[:], p_aT[0:GS, 0:NG * GS]).then_inc(a_aT, 1)
                if exists(t, E):
                    wait(act, m_qk, t + 1)
                    wait(act, m_s, t - 1)
                    nc.scalar.copy(view(qk[j], 2 * ROT, P - 2 * ROT, 0, [[NS, 2], [1, NS]]),
                                   view(p_qk, 2 * ROT, P - 2 * ROT, 0, [[512, 2], [1, NS]])).then_inc(a_rest, 1)
                if exists(t - 2, E):
                    wait(act, m_av, t - 1)
                    nc.scalar.copy(avT[:], p_av[:, 0:NS]).then_inc(a_av, 1)
                if exists(t - 1, E):
                    wait(act, d_shift, t)
                    wait(act, m_aT, t - 1)
                    nc.scalar.activation(a_e[:], s_e[:], ACT.Exp, scale=float(HP) ** -0.5).then_inc(a_exp, 1)
                if exists(t, E):
                    wait(act, m_v, t + 1)
                    nc.scalar.copy(v[t % 4][:], p_v[0:GS, :]).then_inc(a_v, 1)
                if exists(t - 2, E):
                    wait(act, m_o, t - 1)
                    for c in range(DC):
                        leave(nc.scalar.copy, t - 2, c).then_inc(a_o, 1)

            run(act, step)

        @block.vector
        def _(dve):
            def times_cosines(t):
                nc.vector.tensor_tensor(view(straight, 0, 2 * ROT, 0, [[NS, 2], [1, NS]]),
                                        view(p_qk, 0, 2 * ROT, 0, [[512, 2], [1, NS]]),
                                        view(slot_angles, 0, 2 * ROT, t * NS, [[0, 2], [1, NS]]),
                                        ALU.mult).then_inc(d_rope, 2)

            def step(t, j):
                if exists(t, E):
                    wait(dve, m_qk, t + 1)
                    wait(dve, g_s, t)
                    for lo, hi in ((0, ROT), (ROT, 0)):
                        nc.vector.tensor_tensor(view(turned, lo, ROT, 0, [[NS, 2], [1, NS]]),
                                                view(p_qk, hi, ROT, 0, [[512, 2], [1, NS]]),
                                                view(slot_angles, 2 * ROT + lo, ROT, t * NS, [[0, 2], [1, NS]]),
                                                ALU.mult).then_inc(d_turn, 1)
                if exists(t, E) and t < 2:
                    times_cosines(t)
                if exists(t - 1, E):
                    u = t - 1
                    wait(dve, m_s, u + 1)
                    wait(dve, a_exp, u)
                    nc.vector.tensor_tensor(view(s_e, 0, GS, 0, [[GS, NG], [1, GS]]),
                                            view(p_s, 0, GS, 0, [[GS, NG], [1, GS]]),
                                            view(consts, 0, GS, C_MASKF, [[0, NG], [1, GS]]),
                                            ALU.add).then_inc(d_mask, 1)
                    wait(dve, d_mask, u + 1)
                    s3 = view(s_e, 0, GS, 0, [[GS, NG], [1, GS]])
                    nc.vector.tensor_reduce(mx[:], s3, AX, ALU.max).then_inc(d_max, 1)
                    wait(dve, d_max, u + 1)
                    nc.vector.tensor_tensor(s3, s3, view(mx, 0, GS, 0, [[1, NG], [0, GS]]),
                                            ALU.subtract).then_inc(d_shift, 1)
                if exists(t, E) and t >= 2:
                    times_cosines(t)
                if exists(t - 1, E):
                    u = t - 1
                    wait(dve, a_exp, u + 1)
                    a3 = view(a_e, 0, GS, 0, [[GS, NG], [1, GS]])
                    nc.vector.tensor_reduce(sm[:], a3, AX, ALU.add).then_inc(d_sum, 1)
                    wait(dve, d_sum, u + 1)
                    nc.vector.reciprocal(inv[:], sm[:]).then_inc(d_inv, 1)
                    wait(dve, d_inv, u + 1)
                    nc.vector.tensor_tensor(a3, a3, view(inv, 0, GS, 0, [[1, NG], [0, GS]]),
                                            ALU.mult).then_inc(d_norm, 1)
            run(dve, step)

        @block.gpsimd
        def _(pool):
            for t in range(E):
                if exists(t + 1, E):
                    wait(pool, m_v, t)
                    expert_weights_low(nc, pool, weights, t + 1)
                wait(pool, d_turn, 2 * (t + 1))
                wait(pool, d_rope, 2 * (t + 1))
                wait(pool, m_s, t - 1)
                nc.gpsimd.tensor_tensor(qk[t % 2][0:2 * ROT, :], straight[:], turned[0:2 * ROT, :],
                                        ALU.add).then_inc(g_s, 1)


def build_scatter(nc, io, consts, h_all, slot_out, chosen_gate):
    with ExitStack() as ctx:
        def sb(name, cols, rows=P):
            return ctx.enter_context(nc.sbuf_tensor(name, [rows, cols], F32))

        def sem(name):
            return ctx.enter_context(nc.semaphore(name))

        ES = E * PS
        outs = [sb(f"outs{j}", QUAD * DC * ES) for j in range(2)]
        gts = [sb(f"gts{j}", QUAD * ES) for j in range(2)]
        back = [sb(f"back{j}", DC * P + P, ES) for j in range(2)]
        final = [sb(f"final{j}", QUAD * D) for j in range(2)]
        p_t = [ctx.enter_context(nc.psum_tensor(f"p_t{j}", [P, 512], F32)) for j in range(2)]
        p_f = [ctx.enter_context(nc.psum_tensor(f"p_f{j}", [P, 512], F32)) for j in range(2)]
        c_in = sem("c_in")
        c_out = [sem(f"c_out{j}") for j in range(2)]
        c_T, c_back, c_mm, c_fin = sem("c_T"), sem("c_back"), sem("c_mm"), sem("c_fin")
        block = ctx.enter_context(nc.Block())

        @block.sync
        def _(sp):
            def store(q, j):
                wait(sp, c_fin, (q + 1) * QUAD)
                for b in range(IMGS):
                    sp.dma_start(io["out"][bass.ds(q * QUAD, QUAD), b].rearrange("q t n -> t q n"),
                                 final[j][b * TP:b * TP + T, :].rearrange("t (q n) -> t q n", q=QUAD)
                                 ).then_inc(c_out[j], 16)

            with sp.Fori(0, NQ // 2) as i:
                for j in range(2):
                    store(i * 2 + j, j)
            for j in range(2):
                sp.wait_ge(c_out[j], 16 * IMGS * NQ // 2)

        def quads(eng, body):
            for q in range(2):
                for k in range(QUAD):
                    body(q, q, k, q * QUAD + k)
            with eng.Fori(1, NQ // 2) as i:
                for j in range(2):
                    for k in range(QUAD):
                        q = i * 2 + j
                        body(q, j, k, q * QUAD + k)

        @block.tensor
        def _(pe):
            ident = consts[:, C_ID:C_ID + P]

            def scatter(u, k):
                wait(pe, c_back, u + 1)
                wait(pe, c_fin, u - 1)
                nc.tensor.matmul(p_f[k % 2][:, 0:D], back[k % 2][:, DC * P:], back[k % 2][:, 0:D],
                                 start=True, stop=True).then_inc(c_mm, 1)

            def body(q, j, k, u):
                if k == 0:
                    wait(pe, c_in, (q + 1) * 2)
                wait(pe, c_back, u - 1)
                for c in range(DC):
                    nc.tensor.transpose(p_t[k % 2][0:ES, c * P:(c + 1) * P],
                                        outs[j][:, (k * DC + c) * ES:(k * DC + c + 1) * ES], ident)
                nc.tensor.transpose(p_t[k % 2][0:ES, DC * P:DC * P + P], gts[j][:, k * ES:(k + 1) * ES],
                                    ident).then_inc(c_T, 1)
                if not (isinstance(u, int) and u == 0):
                    scatter(u - 1, k - 1)

            keep_clock_up(nc, consts, p_f[0], 3)
            quads(pe, body)
            scatter(PAIRS - 1, QUAD - 1)

        @block.scalar
        def _(act):
            def body(q, j, k, u):
                wait(act, c_T, u + 1)
                wait(act, c_mm, u - 1)
                nc.scalar.copy(back[k % 2][:], p_t[k % 2][0:ES, 0:DC * P + P]).then_inc(c_back, 1)

            quads(act, body)

        @block.vector
        def _(dve):
            def fetch(q, j):
                wait(dve, c_T, (q - 1) * QUAD)
                nc.vector.tensor_copy(outs[j][:], slot_out[:, bass.ds(q * (QUAD * DC * ES), QUAD * DC * ES)]
                                      ).then_inc(c_in, 1)
                nc.vector.tensor_copy(gts[j][:], chosen_gate[:, bass.ds(q * (QUAD * ES), QUAD * ES)]
                                      ).then_inc(c_in, 1)

            def body(q, j, k, u, ahead=True):
                if k == 1 and ahead:
                    fetch(q + 1, 1 - j)
                wait(dve, c_mm, u + 1)
                if k == 0:
                    wait(dve, c_out[j], (q - j) * 16)
                nc.vector.tensor_tensor(final[j][:, k * D:(k + 1) * D], p_f[k % 2][:, 0:D],
                                        h_all[:, bass.ds(u * D, D)], ALU.add).then_inc(c_fin, 1)

            fetch(0, 0)
            for q in range(2):
                for k in range(QUAD):
                    body(q, q, k, q * QUAD + k)
            with dve.Fori(1, NQ // 2 - 1) as i:
                for j in range(2):
                    for k in range(QUAD):
                        q = i * 2 + j
                        body(q, j, k, q * QUAD + k)
            for q in range(NQ - 2, NQ):
                for k in range(QUAD):
                    body(q, q % 2, k, q * QUAD + k, ahead=q < NQ - 1)


def build(nc, io):
    with ExitStack() as ctx:
        def sb(name, cols, dtype=F32):
            return ctx.enter_context(nc.sbuf_tensor(name, [P, cols], dtype))

        consts = sb("consts", C_END)
        h_all = sb("h_all", PAIRS * D)
        logits = sb("logits", PAIRS * E)
        build_attention(nc, io, h_all, logits, consts)
        chosen_gate = sb("chosen_gate", PAIRS * E * PS)
        slot_parts = [sb(f"slot_rows_{part}", DC * E * NS, F32R) for part in ("hi", "lo")]
        slot_angles = sb("slot_angles", E * NS)
        weights = ExpertWeights(nc, ctx)
        build_routing(nc, io, logits, consts, weights, chosen_gate, slot_parts, slot_angles)
        slot_out = sb("slot_out", PAIRS * DC * E * PS)
        build_experts(nc, io, consts, weights, slot_parts, slot_angles, slot_out)
        build_scatter(nc, io, consts, h_all, slot_out, chosen_gate)


def constants():
    import numpy as np
    c = np.zeros((P, C_END), np.float32)
    row = np.arange(P)
    tok = (row % TP).astype(np.float32)
    c[:, C_ID:C_ID + P] = np.eye(P)
    inv = np.float32(1.0) / np.power(np.float32(10000.0), np.arange(0, HD, 2, dtype=np.float32) / np.float32(HD))
    ang = tok[:, None] * inv.astype(np.float32)[None]
    c[:, C_COS:C_COS + HD] = np.tile(np.cos(ang), 2)
    c[:, C_SIN:C_SIN + HD] = np.concatenate([-np.sin(ang), np.sin(ang)], 1)
    c[:, C_CAUSAL:C_CAUSAL + T] = np.where(np.arange(T)[None] <= (row % TP)[:, None], 0.0, NEG)
    c[:, C_HEAD:C_HEAD + HC] = (row // HD)[:, None] == np.arange(HC)[None]
    inv = np.float32(1.0) / np.power(np.float32(10000.0),
                                     np.arange(ROT, dtype=np.float32) * np.float32(2.0) / np.float32(2 * ROT))
    ang = tok[:, None] * inv.astype(np.float32)[None]
    c[:, C_ROT:C_ROT + P] = np.concatenate([np.cos(ang), np.cos(ang), -np.sin(ang), np.sin(ang)], 1)
    q, k = np.arange(P)[:, None], np.arange(GS)[None]
    c[:, C_MASKF:C_MASKF + GS] = np.where((q // SLOTS == k // SLOTS) & (k <= q), 0.0, NEG)
    c[:, C_SLOT:C_SLOT + SLOTS] = np.arange(1, SLOTS + 1)
    return c


def kernel(x, L0_tok_W, L0_tok_b, L0_attn_w_qkv, L0_attn_w_proj, L0_attn_b_proj, L0_ffn_Wr, L0_ffn_Wqkv, L0_ffn_Wo):
    import numpy as np
    import concourse.bacc as bacc
    from concourse.bass_utils import run_bass_kernel_spmd

    nc = bacc.Bacc("TRN2", target_bir_lowering=False, num_devices=1)
    xs = np.asarray(x).reshape(PAIRS, IMGS, 3, 7, 16, 7, 16).transpose(0, 2, 4, 6, 1, 3, 5)
    xs = xs.reshape(PAIRS, KC, P, PATCH_COLS).transpose(0, 2, 1, 3).reshape(PAIRS, P, KC * PATCH_COLS)
    router = np.asarray(L0_ffn_Wr).T.reshape(DC, P, E).transpose(1, 0, 2).reshape(P, DC * E)
    arrays = {"patchesT": xs, "routerT": router, "consts": constants(), "L0_tok_W": L0_tok_W, "L0_tok_b": L0_tok_b,
              "L0_attn_w_qkv": L0_attn_w_qkv, "L0_attn_w_proj": L0_attn_w_proj, "L0_attn_b_proj": L0_attn_b_proj,
              "L0_ffn_Wqkv": L0_ffn_Wqkv, "L0_ffn_Wo": L0_ffn_Wo}
    arrays = {n: np.ascontiguousarray(a) for n, a in arrays.items()}
    io = {n: nc.dram_tensor("in_" + n, a.shape, mybir.dt.from_np(a.dtype), kind="ExternalInput").ap()
          for n, a in arrays.items()}
    io["xn2_dram"] = nc.dram_tensor("xn2_dram", (PAIRS, P, D), F32, kind="Internal").ap()
    out = nc.dram_tensor("out_rows", (PAIRS, IMGS, T, D), F32, kind="ExternalOutput").ap()
    io["out"] = out
    build(nc, io)
    r = run_bass_kernel_spmd(nc, [{"in_" + n: a for n, a in arrays.items()}], core_ids=[0])
    return r.results[0]["out_rows"].reshape(PAIRS * IMGS, T, D)
```
